# Optimizing a Trainium2 kernel written in Bass

```python
import numpy as np
import jax
import jax.numpy as jnp

def _softmax(x, axis=-1):
    return jax.nn.softmax(x, axis=axis)

def _gelu(x):
    return jax.nn.gelu(x, approximate=True)

def _silu(x):
    return jax.nn.silu(x)

def _sigmoid(x):
    return jax.nn.sigmoid(x)

def _layernorm(x, axis=-1, eps=1e-05):
    m = jnp.mean(x, axis=axis, keepdims=True)
    v = jnp.var(x, axis=axis, keepdims=True)
    return (x - m) / jnp.sqrt(v + eps)

def _scatter_add(tgt, idx, src, axis=0):
    return tgt.at[idx].add(src)

def _segment_sum(src, seg, n):
    return jax.ops.segment_sum(src, seg, n)
kernel_name = 'mk_macaron_d1_jaxref_r8_cd50b3'

def setup_inputs(seed: int=0):
    np.random.seed(seed)
    _w = jnp.asarray

    def _L0_attn_setup():
        import jax, jax.numpy as jnp
        import numpy as np
        B, S, D = (4, 256, 128)

        def _wkv(k, v, time_decay, u):
            w = -jnp.exp(time_decay)
            b, s, d = k.shape
            aa = jnp.zeros((b, d), k.dtype)
            bb = jnp.zeros((b, d), k.dtype)
            pp = jnp.full((b, d), -1e+30, k.dtype)

            def step(carry, kv):
                aa, bb, pp = carry
                kk, vv = kv
                ww = u + kk
                p = jnp.maximum(pp, ww)
                e1 = jnp.exp(pp - p)
                e2 = jnp.exp(ww - p)
                out = (e1 * aa + e2 * vv) / (e1 * bb + e2)
                ww2 = w + pp
                p2 = jnp.maximum(ww2, kk)
                e1b = jnp.exp(ww2 - p2)
                e2b = jnp.exp(kk - p2)
                return ((e1b * aa + e2b * vv, e1b * bb + e2b, p2), out)
            _, outs = jax.lax.scan(step, (aa, bb, pp), (k.transpose(1, 0, 2), v.transpose(1, 0, 2)))
            return outs.transpose(1, 0, 2)
        key = jax.random.key(seed)
        ks = jax.random.split(key, 10)
        s = 0.02
        return {'x': jax.random.normal(ks[0], (B, S, D), jnp.float32), 'time_mix_k': jax.random.uniform(ks[1], (1, 1, D), jnp.float32), 'time_mix_v': jax.random.uniform(ks[2], (1, 1, D), jnp.float32), 'time_mix_r': jax.random.uniform(ks[3], (1, 1, D), jnp.float32), 'time_decay': jax.random.normal(ks[4], (D,), jnp.float32) * 0.1, 'time_first': jax.random.normal(ks[5], (D,), jnp.float32) * 0.1, 'Wk': jax.random.normal(ks[6], (D, D), jnp.float32) * s, 'Wv': jax.random.normal(ks[7], (D, D), jnp.float32) * s, 'Wr': jax.random.normal(ks[8], (D, D), jnp.float32) * s, 'Wo': jax.random.normal(ks[9], (D, D), jnp.float32) * s}
    _L0_attn_in = _L0_attn_setup()

    def _L0_ffn_setup():
        import jax, jax.numpy as jnp
        import numpy as np
        TOP_K = 2
        key = jax.random.key(seed)
        ks = jax.random.split(key, 5)
        B, T, D, F, E = (4, 256, 128, 512, 8)
        s = 0.02
        return {'x': jax.random.normal(ks[0], (B, T, D), jnp.float32), 'gate_w': jax.random.normal(ks[1], (D, E), jnp.float32) * s, 'w1': jax.random.normal(ks[2], (E, D, F), jnp.float32) * s, 'w3': jax.random.normal(ks[3], (E, D, F), jnp.float32) * s, 'w2': jax.random.normal(ks[4], (E, F, D), jnp.float32) * s}
    _L0_ffn_in = _L0_ffn_setup()
    _d = {'L0_attn_x': _L0_attn_in['x'], 'L0_attn_time_mix_k': _L0_attn_in['time_mix_k'], 'L0_attn_time_mix_v': _L0_attn_in['time_mix_v'], 'L0_attn_time_mix_r': _L0_attn_in['time_mix_r'], 'L0_attn_time_decay': _L0_attn_in['time_decay'], 'L0_attn_time_first': _L0_attn_in['time_first'], 'L0_attn_Wk': _L0_attn_in['Wk'], 'L0_attn_Wv': _L0_attn_in['Wv'], 'L0_attn_Wr': _L0_attn_in['Wr'], 'L0_attn_Wo': _L0_attn_in['Wo'], 'L0_ffn_gate_w': _L0_ffn_in['gate_w'], 'L0_ffn_w1': _L0_ffn_in['w1'], 'L0_ffn_w3': _L0_ffn_in['w3'], 'L0_ffn_w2': _L0_ffn_in['w2']}
    _x0 = _d['L0_attn_x']
    _d['L0_attn_x'] = jax.random.normal(jax.random.fold_in(jax.random.key(seed), 1), (8, 512, 128), dtype=_x0.dtype)
    del _x0
    return _d

def reference(L0_attn_x, L0_attn_time_mix_k, L0_attn_time_mix_v, L0_attn_time_mix_r, L0_attn_time_decay, L0_attn_time_first, L0_attn_Wk, L0_attn_Wv, L0_attn_Wr, L0_attn_Wo, L0_ffn_gate_w, L0_ffn_w1, L0_ffn_w3, L0_ffn_w2):

    def _L0_attn_ref(x, time_mix_k, time_mix_v, time_mix_r, time_decay, time_first, Wk, Wv, Wr, Wo):
        import jax, jax.numpy as jnp
        import numpy as np
        B, S, D = (4, 256, 128)

        def _wkv(k, v, time_decay, u):
            w = -jnp.exp(time_decay)
            b, s, d = k.shape
            aa = jnp.zeros((b, d), k.dtype)
            bb = jnp.zeros((b, d), k.dtype)
            pp = jnp.full((b, d), -1e+30, k.dtype)

            def step(carry, kv):
                aa, bb, pp = carry
                kk, vv = kv
                ww = u + kk
                p = jnp.maximum(pp, ww)
                e1 = jnp.exp(pp - p)
                e2 = jnp.exp(ww - p)
                out = (e1 * aa + e2 * vv) / (e1 * bb + e2)
                ww2 = w + pp
                p2 = jnp.maximum(ww2, kk)
                e1b = jnp.exp(ww2 - p2)
                e2b = jnp.exp(kk - p2)
                return ((e1b * aa + e2b * vv, e1b * bb + e2b, p2), out)
            _, outs = jax.lax.scan(step, (aa, bb, pp), (k.transpose(1, 0, 2), v.transpose(1, 0, 2)))
            return outs.transpose(1, 0, 2)
        shifted = jnp.concatenate([jnp.zeros_like(x[:, :1, :]), x[:, :-1, :]], axis=1)
        xk = x * time_mix_k + shifted * (1.0 - time_mix_k)
        xv = x * time_mix_v + shifted * (1.0 - time_mix_v)
        xr = x * time_mix_r + shifted * (1.0 - time_mix_r)
        k = jnp.einsum('bsd,ed->bse', xk, Wk)
        v = jnp.einsum('bsd,ed->bse', xv, Wv)
        r = jax.nn.sigmoid(jnp.einsum('bsd,ed->bse', xr, Wr))
        wkv = _wkv(k, v, time_decay, time_first)
        out = jnp.einsum('bsd,ed->bse', r * wkv, Wo)
        return out

    def _L0_ffn_ref(x, gate_w, w1, w3, w2):
        import jax, jax.numpy as jnp
        import numpy as np
        TOP_K = 2
        logits = jnp.einsum('btd,de->bte', x, gate_w)
        probs = jax.nn.softmax(logits, axis=-1)
        expert_weights, expert_indices = jax.lax.top_k(probs, TOP_K)
        expert_weights = expert_weights / expert_weights.sum(-1, keepdims=True)
        E = w1.shape[0]
        out = jnp.zeros_like(x)
        for i in range(E):
            wi = jnp.where(expert_indices == i, expert_weights, 0.0).sum(-1)
            h = jax.nn.silu(jnp.einsum('btd,df->btf', x, w1[i])) * jnp.einsum('btd,df->btf', x, w3[i])
            out = out + jnp.einsum('btf,fd->btd', h, w2[i]) * wi[..., None]
        return out
    x = L0_attn_x
    x = x + 0.5 * _L0_ffn_ref(_layernorm(x, axis=-1), L0_ffn_gate_w, L0_ffn_w1, L0_ffn_w3, L0_ffn_w2)
    x = x + _L0_attn_ref(_layernorm(x, axis=-1), L0_attn_time_mix_k, L0_attn_time_mix_v, L0_attn_time_mix_r, L0_attn_time_decay, L0_attn_time_first, L0_attn_Wk, L0_attn_Wv, L0_attn_Wr, L0_attn_Wo)
    x = x + 0.5 * _L0_ffn_ref(_layernorm(x, axis=-1), L0_ffn_gate_w, L0_ffn_w1, L0_ffn_w3, L0_ffn_w2)
    return x

_drawn_inputs = setup_inputs


def setup_inputs(seed=0):
    import zlib

    import numpy as np

    out = dict(_drawn_inputs(seed))
    spreads = {}
    factors = {'L0_attn_time_mix_k': 8.0,
     'L0_attn_time_mix_v': 8.0,
     'L0_attn_time_mix_r': 8.0,
     'L0_attn_time_decay': 8.0,
     'L0_attn_time_first': 8.0,
     'L0_attn_Wk': 8.0,
     'L0_attn_Wv': 4.048,
     'L0_attn_Wr': 8.0,
     'L0_attn_Wo': 4.162,
     'L0_ffn_gate_w': 7.76,
     'L0_ffn_w1': 6.832,
     'L0_ffn_w3': 6.801,
     'L0_ffn_w2': 6.792}
    for name, (base, spread) in spreads.items():
        noise = np.random.default_rng([zlib.crc32(name.encode()), seed]).standard_normal(out[name].shape)
        drawn = base * np.exp(spread * noise) if base else spread * noise
        out[name] = jnp.asarray(drawn.astype(out[name].dtype))
    for name, factor in factors.items():
        out[name] = (out[name] * factor).astype(out[name].dtype)
    return out
```

```python
from contextlib import ExitStack

import concourse.bass as bass
from concourse import mybir

ALU = mybir.AluOpType
ACT = mybir.ActivationFunctionType
AX = mybir.AxisListType
F32 = mybir.dt.float32
F16 = mybir.dt.float16
BF16 = mybir.dt.bfloat16
I32 = mybir.dt.int32
U8 = mybir.dt.uint8

P = 128
B, S, D = 8, 512, 128
E, F, TOPK = 8, 512, 2
FC = F // P
JU = S // P
GROUPS = 2
UG = B // GROUPS
JG = UG * JU
GTOK = JG * P
T = 256
TH = T // P
NT = (GTOK * TOPK + E * (T - 1)) // T
EPS = 1e-5
WS = 64.0
MAGIC = 0x5F3759DF
NEG = -1e30
BIG = 3e38

STAGES = [("route", 0, 0), ("route", 1, 0), ("ffn", 0, 0), ("ffn", 1, 0),
          ("mix", 0, 0), ("route", 0, 1), ("mix", 1, 0), ("route", 1, 1),
          ("ffn", 0, 1), ("ffn", 1, 1), ("last", 0, 1), ("last", 1, 1)]


def before(stage, per):
    return sum(per.get(s[0], 0) for s in STAGES[:STAGES.index(stage)])


def macaron_kernel(nc, x, channel_vecs, att_w, gate, w1, w3, w2, out):
    with ExitStack() as ctx:
        def sb(name, shape, dt=F32):
            return ctx.enter_context(nc.sbuf_tensor(name, shape, dt))

        def ps(name, shape, dt=F32):
            return ctx.enter_context(nc.psum_tensor(name, shape, dt))

        def sem(name):
            return ctx.enter_context(nc.semaphore(name))

        rows_in = [nc.dram_tensor(f"rows_in{g}", (NT * T, 2 * D), F16, kind="Internal").ap() for g in range(GROUPS)]
        rows_out = [nc.dram_tensor(f"rows_out{g}", (NT * T, D), F32, kind="Internal").ap() for g in range(GROUPS)]

        xres = sb("xres", [P, GROUPS * JG, D])
        up_w = sb("up_w", [P, E, 4, F], F16)
        down_w = sb("down_w", [P, E, FC, D])
        stage_w = sb("stage_w", [P, 2, F])
        gate_w = sb("gate_w", [P, E])
        att_raw = sb("att_raw", [P, 4, D])
        qkv_f = sb("qkv_f", [P, 6, D])
        qkv_w = sb("qkv_w", [P, 6, 2, D], F16)
        vecs = sb("vecs", [P, 5])
        omix = sb("omix", [P, 3])
        wdec = sb("wdec", [P, 2])
        wfull = sb("wfull", [P, S])
        ident = sb("ident", [P, P])
        ident16 = sb("ident16", [P, P], F16)
        upper = sb("upper", [P, P], BF16)
        ones16 = sb("ones16", [P, P], BF16)
        zrow = sb("zrow", [P, 2 * D], F16)
        e_desc = sb("e_desc", [P, JG, E])
        t_iota = sb("t_iota", [P, NT, E])
        stats = sb("stats", [P, JU, 6])
        mv = sb("mv", [P, JU, 2])
        var = sb("var", [P, JU])
        bits = sb("bits", [P, JU], I32)
        rstd = sb("rstd", [P, JU])
        nwt = sb("nwt", [P, JU])
        xn = sb("xn", [P, 2, JU, D])
        parts = sb("parts", [P, GROUPS, JG, 2 * D], F16)
        xnT = sb("xnT", [P, S])
        logit = sb("logit", [P, JG, E])
        rt = [sb(f"rt{i}", [P, JG, E]) for i in range(3)]
        pick = [sb(f"pick{i}", [P, JG, E]) for i in range(2)]
        mx = [sb(f"mx{i}", [P, JG]) for i in range(2)]
        kx = sb("kx", [P, JG])
        chosen = sb("chosen", [P, JG, E], BF16)
        cnt = sb("cnt", [P, E, JG])
        run = sb("run", [P, E, JG])
        one_s = sb("one_s", [P, E * JG])
        ne = sb("ne", [P, 6, E])
        nei = sb("nei", [P, E], I32)
        tcmp = sb("tcmp", [P, NT, E])
        teid = sb("teid", [P, NT + 2])
        slotf = sb("slotf", [P, 2, JG])
        slot = sb("slot", [P, GROUPS, 2, JG], I32)
        wts = sb("wts", [P, GROUPS, 2, JG])
        ed = sb("ed", [P, 2, JG])
        eid = sb("eid", [P, GROUPS, NT + 1], I32)
        rin = sb("rin", [P, 2, TH, 2 * D], F16)
        rT = sb("rT", [P, 2, 2, T], F16)
        sil = sb("sil", [P, 2, 2 * T])
        h = sb("h", [P, 2, FC, T])
        yrow = sb("yrow", [P, 2, TH, D])
        yg = sb("yg", [P, 2, 2, JU, D])
        xT = sb("xT", [P, 2, 2, S + 2], F16)
        kk = sb("kk", [P, 2, S])
        vv = sb("vv", [P, 2, S])
        er = sb("er", [P, 2, S])
        pp = sb("pp", [P, S + 1])
        dd = sb("dd", [P, S])
        mn = sb("mn", [P, 2, S])
        mxx = sb("mxx", [P, 2, S])
        e1 = sb("e1", [P, 2, S])
        e2 = sb("e2", [P, 2, S])
        kv = sb("kv", [P, S])
        aa = sb("aa", [P, S + 1])
        bb = sb("bb", [P, S + 1])
        num = sb("num", [P, S])
        den = sb("den", [P, S])
        tm = sb("tm", [P, S])
        att = sb("att", [P, S])

        pa = [ps(f"pa{q}", [P, 2 * T]) for q in range(2)]
        pb = [ps(f"pb{q}", [P, 2 * T]) for q in range(2)]
        pT = ps("pT", [P, 2, T], F16)
        py = ps("py", [P, TH, D])
        bkA = ps("bkA", [P, S])
        bkB = ps("bkB", [P, S])

        s_x = [sem(f"x_in{g}") for g in range(GROUPS)]
        s_small = sem("small_in")
        s_stage = [sem(f"stage_in{i}") for i in range(2)]
        s_w2 = sem("w2_in")
        s_zrow = sem("zrow_made")
        s_fill = [sem(f"rows_zeroed{g}") for g in range(GROUPS)]
        s_const = sem("const_made")
        s_uphi = sem("up_hi_made")
        s_uplo = sem("up_lo_made")
        s_qf = sem("qkv_folded")
        s_qhi = sem("qkv_hi_made")
        s_qlo = sem("qkv_lo_made")
        s_wexp = sem("decay_exp_made")
        s_chain = sem("dve_chain")
        s_xn = sem("xn_made")
        s_hi = sem("parts_hi_made")
        s_lo = sem("parts_lo_made")
        s_afull = sem("bankA_full")
        s_aread = sem("bankA_read")
        s_bfull = sem("bankB_full")
        s_bread = sem("bankB_read")
        s_gap = sem("logit_gap_made")
        s_ed = sem("gap_exp_made")
        s_chosen = sem("chosen_made")
        s_routed = sem("routed")
        s_scat = [sem(f"scattered{g}") for g in range(GROUPS)]
        s_rin = [sem(f"tile_in{i}") for i in range(2)]
        s_turn = sem("tile_turned")
        s_rT = sem("tile_copied")
        s_up = sem("up_done")
        s_sil = sem("silu_done")
        s_h = sem("h_made")
        s_y = sem("down_done")
        s_yrow = sem("y_copied")
        s_yst = [sem(f"y_stored{i}") for i in range(2)]
        s_gat = [sem(f"gathered{i}") for i in range(2)]
        s_comb = sem("combined")
        s_min = sem("minmax_made")
        s_exp = sem("exps_made")
        s_att = sem("att_made")
        s_out = sem("out_stored")

        block = ctx.enter_context(nc.Block())

        A_ORDER = {"route": [f"turn{b}" for b in range(UG)] + ["prefix"],
                   "mix": ["turn0", "v0"] + [x + str(b) for b in range(1, UG) for x in ("turn", "out-", "v")]
                   + [f"out{UG - 1}"]}
        A_ORDER["mix"] = [f"out{int(x[4:]) - 1}" if x.startswith("out-") else x for x in A_ORDER["mix"]]
        B_ORDER = {"route": [f"logits{b}" for b in range(UG)] + ["totals"],
                   "mix": [x + str(b) for b in range(UG) for x in ("k", "r")]}
        A_USES = {kind: len(o) for kind, o in A_ORDER.items()}
        B_USES = {kind: len(o) for kind, o in B_ORDER.items()}
        NORMS = {"route": UG, "mix": UG}
        COMBINES = {"mix": UG, "last": UG}
        ROUTES, RUNS, TILES = {"route": 1}, {"ffn": 1}, {"ffn": NT}
        MIXES = {"mix": UG}
        SLOT_TILES = [(NT + 1) // 2, NT // 2]

        def a_use(stage, name):
            return before(stage, A_USES) + A_ORDER[stage[0]].index(name) + 1

        def b_use(stage, name):
            return before(stage, B_USES) + B_ORDER[stage[0]].index(name) + 1

        def each_tile(eng, body):
            body(0, 0, None)
            with eng.Fori(0, NT // 2 - 1) as i:
                body(2 * i + 1, 1, i)
                body(2 * i + 2, 0, i)
            body(NT - 2, 1, NT // 2 - 1)
            body(NT - 1, 0, NT // 2 - 1)

        @block.sync
        def _(sp):
            xv = x.rearrange("b (j p) d -> p (b j) d", p=P)
            ov = out.rearrange("b (j p) d -> p (b j) d", p=P)
            sp.dma_start(xres[:, 0:JG, :], xv[:, 0:JG, :]).then_inc(s_x[0], 16)
            sp.dma_start(gate_w[:], gate).then_inc(s_small, 16)
            sp.dma_start(vecs[:], channel_vecs).then_inc(s_small, 16)
            sp.dma_start(att_raw[:], att_w).then_inc(s_small, 16)
            sp.wait_ge(s_zrow, 1)
            sp.dma_start(rows_in[0].rearrange("(p r) c -> p r c", p=P),
                         zrow[:, None, :].to_broadcast([P, NT * T // P, 2 * D])).then_inc(s_fill[0], 16)
            sp.dma_start(xres[:, JG:, :], xv[:, JG:, :]).then_inc(s_x[1], 16)
            with sp.Fori(0, E) as e:
                for i, a in enumerate((w1, w3)):
                    sp.wait_ge(s_uplo, 2 * e + i + 1)
                    sp.dma_start(stage_w[:, i, :], a[bass.ds(e, 1), :, :].rearrange("e d f -> d (e f)")
                                 ).then_inc(s_stage[i], 16)
            sp.dma_start(down_w[:], w2.rearrange("e (c p) d -> p e c d", p=P)).then_inc(s_w2, 16)
            sp.dma_start(rows_in[1].rearrange("(p r) c -> p r c", p=P),
                         zrow[:, None, :].to_broadcast([P, NT * T // P, 2 * D])).then_inc(s_fill[1], 16)

            for stage in STAGES:
                kind, g, l = stage
                if kind == "ffn":
                    n0 = before(stage, TILES)

                    def load(t, k):
                        sp.wait_ge(s_turn, n0 + t + 1)
                        sp.dma_start(rin[:, k, :, :],
                                     rows_in[g][bass.ds(t * T, T), :].rearrange("(h p) c -> p h c", p=P)
                                     ).then_inc(s_rin[k], 16)

                    def store(t, k):
                        sp.wait_ge(s_yrow, n0 + t + 3)
                        sp.dma_start(rows_out[g][bass.ds(t * T, T), :].rearrange("(h p) c -> p h c", p=P),
                                     yrow[:, k, :, :]).then_inc(s_yst[k], 16)

                    sp.wait_ge(s_scat[g], 16 * TOPK * JG * (l + 1))
                    load(0, 0)
                    load(1, 1)
                    load(2, 0)
                    with sp.Fori(0, NT // 2 - 1) as i:
                        load(2 * i + 3, 1)
                        store(2 * i, 0)
                        load(2 * i + 4, 0)
                        store(2 * i + 1, 1)
                    for t in range(NT - 3, NT):
                        store(t, t % 2)
                if kind == "last":
                    for b in range(UG):
                        u = g * UG + b
                        sp.wait_ge(s_comb, before(stage, COMBINES) + b + 1)
                        sp.dma_start(ov[:, u * JU:(u + 1) * JU, :], xres[:, u * JU:(u + 1) * JU, :]
                                     ).then_inc(s_out, 16)
            sp.wait_ge(s_out, 16 * B)

        @block.gpsimd
        def _(pool):
            pool.memset(ident[:], 0.0).then_inc(s_const, 1)
            pool.memset(upper[:], 0.0).then_inc(s_const, 1)
            pool.wait_ge(s_const, 2)
            pool.affine_select(out=ident[:], in_=ident[:], compare_op=ALU.not_equal, fill=1.0, base=0,
                               pattern=[[-1, P]], channel_multiplier=1).then_inc(s_const, 1)
            pool.affine_select(out=upper[:], in_=upper[:], compare_op=ALU.is_ge, fill=1.0, base=0,
                               pattern=[[-1, P]], channel_multiplier=1).then_inc(s_const, 1)
            pool.wait_ge(s_const, 4)
            pool.tensor_copy(ident16[:], ident[:]).then_inc(s_const, 1)
            pool.iota(e_desc[:], [[0, JG], [-1, E]], E, 0, allow_small_or_imprecise_dtypes=True).then_inc(s_const, 1)
            pool.iota(t_iota[:], [[1, NT], [0, E]], 0, 0, allow_small_or_imprecise_dtypes=True).then_inc(s_const, 1)
            for stage in STAGES:
                kind, g, l = stage
                if kind == "route":
                    pool.wait_ge(s_routed, before(stage, ROUTES) + 1)
                    pool.wait_ge(s_lo, before(stage, NORMS) + UG)
                    if l == 0:
                        pool.wait_ge(s_fill[g], 16)
                    for j in range(JG):
                        for c in range(TOPK):
                            pool.indirect_dma_start(
                                rows_in[g][:], bass.IndirectOffsetOnAxis(ap=slot[:, g, c, j:j + 1], axis=0),
                                parts[:, g, j, :], None).then_inc(s_scat[g], 16)
                if kind in ("mix", "last"):
                    runs = before(("ffn", g, l), RUNS) + 1
                    for k in range(2):
                        pool.wait_ge(s_yst[k], 16 + 16 * SLOT_TILES[k] * runs)
                    for b in range(UG):
                        c0 = before(stage, COMBINES) + b
                        if c0 >= 2:
                            pool.wait_ge(s_comb, c0 - 1)
                        for j in range(JU):
                            for c in range(TOPK):
                                pool.indirect_dma_start(
                                    yg[:, b % 2, c, j, :], None, rows_out[g][:],
                                    bass.IndirectOffsetOnAxis(ap=slot[:, g, c, b * JU + j:b * JU + j + 1], axis=0)
                                ).then_inc(s_gat[b % 2], 16)

        @block.scalar
        def _(act):
            act.sem_inc(s_yrow, 2)
            act.sem_inc(s_yst[0], 16)
            act.sem_inc(s_yst[1], 16)
            act.wait_ge(s_small, 16 * 3)
            act.activation(wdec[:, 0:1], vecs[:, 3:4], ACT.Exp).then_inc(s_wexp, 1)

            def split_weights():
                with act.Fori(0, E) as e:
                    for i in range(2):
                        act.wait_ge(s_stage[i], 16 * e + 16)
                        act.activation(up_w[:, bass.ds(e, 1), 2 * i, :].rearrange("p e f -> p (e f)"),
                                       stage_w[:, i, :], ACT.Copy, scale=WS).then_inc(s_uphi, 1)
                act.wait_ge(s_qf, 1)
                act.activation(qkv_w[:, :, 0, :], qkv_f[:], ACT.Copy, scale=WS).then_inc(s_qhi, 1)

            def parts_hi(stage, b):
                u, g = before(stage, NORMS) + b, stage[1]
                act.wait_ge(s_xn, u + 1)
                act.activation(parts[:, g, b * JU:(b + 1) * JU, 0:D], xn[:, u % 2, :, :], ACT.Copy).then_inc(s_hi, 1)

            def route(stage):
                for b in range(UG):
                    parts_hi(stage, b)
                    act.wait_ge(s_afull, a_use(stage, f"turn{b}"))
                    act.activation(xnT[:], bkA[:], ACT.Copy).then_inc(s_aread, 1)
                    act.wait_ge(s_bfull, b_use(stage, f"logits{b}"))
                    act.activation(logit[:, b * JU:(b + 1) * JU, :],
                                   bkB[:, 0:JU * E].rearrange("p (j e) -> p j e", e=E), ACT.Copy).then_inc(s_bread, 1)
                act.wait_ge(s_gap, before(stage, ROUTES) + 1)
                act.activation(ed[:, 0, :], ed[:, 1, :], ACT.Exp).then_inc(s_ed, 1)

            def ffn(stage):
                n0, run_no = before(stage, TILES), before(stage, RUNS)

                def copy_y(t, k, m):
                    act.wait_ge(s_y, n0 + t + 3)
                    act.wait_ge(s_yst[k], 16 * (SLOT_TILES[k] * run_no + m + 1))
                    act.activation(yrow[:, k, :, :], py[:], ACT.Copy).then_inc(s_yrow, 1)

                def tile(t, k, i):
                    for q in range(2):
                        act.wait_ge(s_up, 2 * (n0 + t) + q + 5)
                        act.activation(sil[:, q, :], pa[q][:], ACT.Silu, scale=1.0 / WS).then_inc(s_sil, 1)
                    if i is not None:
                        copy_y(t - 1, 1 - k, i)

                each_tile(act, tile)
                copy_y(NT - 1, 0, NT // 2)

            def mix(stage):
                g, m0 = stage[1], before(stage, MIXES)

                def turn(b):
                    parts_hi(stage, b)
                    act.wait_ge(s_afull, a_use(stage, f"turn{b}"))
                    act.activation(xT[:, b % 2, :, 2:S + 2], bkA[:].bitcast(F16).rearrange("p (h s) -> p h s", h=2),
                                   ACT.Copy).then_inc(s_aread, 1)

                turn(0)
                for b in range(UG):
                    if m0 + b >= 2:
                        act.wait_ge(s_att, m0 + b - 1)
                    act.wait_ge(s_bfull, b_use(stage, f"k{b}"))
                    act.activation(kk[:, b % 2, :], bkB[:], ACT.Copy, scale=1.0 / WS).then_inc(s_bread, 1)
                    act.wait_ge(s_afull, a_use(stage, f"v{b}"))
                    act.activation(vv[:, b % 2, :], bkA[:], ACT.Copy, scale=1.0 / WS).then_inc(s_aread, 1)
                    act.wait_ge(s_bfull, b_use(stage, f"r{b}"))
                    act.activation(er[:, b % 2, :], bkB[:], ACT.Exp, scale=-1.0 / WS).then_inc(s_bread, 1)
                    if b + 1 < UG:
                        turn(b + 1)
                    act.wait_ge(s_min, m0 + b + 1)
                    act.activation(e1[:], mn[:], ACT.Exp).then_inc(s_exp, 1)
                    act.activation(e2[:], mxx[:], ACT.Exp, scale=-1.0).then_inc(s_exp, 1)

            for stage in STAGES:
                if stage[0] == "route":
                    route(stage)
                if stage[0] == "ffn":
                    ffn(stage)
                if stage[0] == "mix":
                    mix(stage)
                if stage == STAGES[0]:
                    split_weights()

        @block.vector
        def _(dve):
            chained = [0]

            def link(ins):
                chained[0] += 1
                ins.then_inc(s_chain, 1)
                dve.wait_ge(s_chain, chained[0])

            dve.sem_inc(s_uplo, 2)
            dve.sem_inc(s_rT, 2)
            dve.sem_inc(s_h, 2)
            dve.memset(zrow[:], 0.0).then_inc(s_zrow, 1)
            dve.memset(ones16[:], 1.0)
            dve.memset(one_s[:], 1.0)
            dve.memset(pp[:, 0:1], NEG)
            dve.memset(aa[:, 0:1], 0.0)
            dve.memset(bb[:, 0:1], 0.0)
            dve.memset(wfull[:], 0.0)
            dve.memset(teid[:], 0.0)
            link(dve.memset(xT[:, :, :, 0:2], 0.0))

            def normalise(stage, b):
                u, g = before(stage, NORMS) + b, stage[1]
                j0 = (g * UG + b) * JU
                for j in range(JU):
                    ins = dve.bn_stats(stats[:, j, :], xres[:, j0 + j, :])
                link(ins)
                for j in range(JU):
                    ins = dve.bn_aggr(mv[:, j, :], stats[:, j, :])
                link(ins)
                link(dve.tensor_scalar(var[:], mv[:, :, 1], EPS, None, ALU.add))
                link(dve.tensor_scalar(bits[:], var[:].bitcast(I32), 1, None, ALU.logical_shift_right))
                link(dve.tensor_scalar(rstd[:].bitcast(I32), bits[:], -1.0, float(MAGIC), ALU.mult, ALU.add))
                for _ in range(3):
                    link(dve.tensor_tensor(nwt[:], rstd[:], rstd[:], ALU.mult))
                    link(dve.scalar_tensor_tensor(nwt[:], nwt[:], -0.5, var[:], ALU.mult, ALU.mult))
                    link(dve.scalar_tensor_tensor(rstd[:], nwt[:], 1.5, rstd[:], ALU.add, ALU.mult))
                if u >= 2:
                    dve.wait_ge(s_hi, u - 1)
                    if stage[0] == "route" and b >= 2:
                        dve.wait_ge(s_afull, a_use(stage, f"turn{b - 2}"))
                for j in range(JU):
                    ins = dve.tensor_scalar(xn[:, u % 2, j, :], xres[:, j0 + j, :], mv[:, j, 0:1], rstd[:, j:j + 1],
                                            ALU.subtract, ALU.mult)
                ins.then_inc(s_xn, 1)

            def parts_lo(stage, b):
                u, g = before(stage, NORMS) + b, stage[1]
                js = slice(b * JU, (b + 1) * JU)
                dve.wait_ge(s_xn, u + 1)
                dve.wait_ge(s_hi, u + 1)
                dve.tensor_tensor(parts[:, g, js, D:2 * D], xn[:, u % 2, :, :], parts[:, g, js, 0:D],
                                  ALU.subtract).then_inc(s_lo, 1)

            def per_token(v):
                return v[:, :, None].to_broadcast([P, JG, E])

            def route(stage):
                g, l = stage[1:]
                if l == 0:
                    dve.wait_ge(s_x[g], 16)
                normalise(stage, 0)
                for b in range(UG):
                    if b + 1 < UG:
                        normalise(stage, b + 1)
                    parts_lo(stage, b)
                dve.wait_ge(s_const, 7)
                dve.wait_ge(s_bread, b_use(stage, f"logits{UG - 1}"))
                src = logit
                for c in range(TOPK):
                    link(dve.tensor_reduce(mx[c][:], src[:], AX.X, ALU.max))
                    link(dve.tensor_tensor(rt[1][:], src[:], per_token(mx[c]), ALU.is_equal))
                    link(dve.tensor_tensor(rt[1][:], rt[1][:], e_desc[:], ALU.mult))
                    link(dve.tensor_reduce(kx[:], rt[1][:], AX.X, ALU.max))
                    link(dve.tensor_tensor(pick[c][:], e_desc[:], per_token(kx), ALU.is_equal))
                    if c == 0:
                        link(dve.scalar_tensor_tensor(rt[0][:], pick[0][:], -BIG, logit[:], ALU.mult, ALU.add))
                        src = rt[0]
                if before(stage, ROUTES):
                    dve.wait_ge(s_ed, before(stage, ROUTES))
                dve.tensor_tensor(ed[:, 1, :], mx[1][:], mx[0][:], ALU.subtract).then_inc(s_gap, 1)
                dve.tensor_tensor(chosen[:], pick[0][:], pick[1][:], ALU.add).then_inc(s_chosen, 1)
                dve.wait_ge(s_bfull, b_use(stage, "totals"))
                link(dve.tensor_copy(cnt[:], bkB[:, 0:JG * E].rearrange("p (j e) -> p e j", e=E)))
                dve.sem_inc(s_bread, 1)
                link(dve.tensor_tensor_scan(run[:].rearrange("p e j -> p (e j)"), one_s[:],
                                            cnt[:].rearrange("p e j -> p (e j)"), 0.0, ALU.mult, ALU.add))
                link(dve.tensor_reduce(ne[:, 0, :], cnt[:], AX.X, ALU.add))
                link(dve.tensor_scalar(nei[:], ne[:, 0, :], float(T - 1), None, ALU.add))
                link(dve.tensor_scalar(nei[:], nei[:], T.bit_length() - 1, None, ALU.logical_shift_right))
                link(dve.tensor_copy(ne[:, 1, :], nei[:]))
                link(dve.tensor_tensor_scan(ne[:, 2, :], one_s[:, 0:E], ne[:, 1, :], 0.0, ALU.mult, ALU.add))
                link(dve.tensor_tensor(ne[:, 3, :], ne[:, 2, :], ne[:, 1, :], ALU.subtract))
                link(dve.tensor_tensor(ne[:, 4, :], run[:, :, JG - 1], ne[:, 0, :], ALU.subtract))
                link(dve.scalar_tensor_tensor(ne[:, 5, :], ne[:, 3, :], float(T), ne[:, 4, :], ALU.mult, ALU.subtract))
                link(dve.tensor_tensor(run[:], run[:], cnt[:], ALU.subtract))
                link(dve.tensor_tensor(run[:], run[:], ne[:, 5, :, None].to_broadcast([P, E, JG]), ALU.add))
                dve.wait_ge(s_afull, a_use(stage, "prefix"))
                link(dve.tensor_tensor(rt[0][:], bkA[:, 0:JG * E].rearrange("p (j e) -> p j e", e=E),
                                       run[:].rearrange("p e j -> p j e"), ALU.add))
                dve.sem_inc(s_aread, 1)
                for c in range(TOPK):
                    link(dve.tensor_tensor(rt[1 + c][:], rt[0][:], pick[c][:], ALU.mult))
                for c in range(TOPK):
                    link(dve.tensor_reduce(slotf[:, c, :], rt[1 + c][:], AX.X, ALU.add))
                dve.tensor_copy(slot[:, g, :, :], slotf[:])
                link(dve.tensor_tensor(tcmp[:], t_iota[:], ne[:, 2, None, :].to_broadcast([P, NT, E]), ALU.is_ge))
                link(dve.tensor_reduce(teid[:, 1:NT + 1], tcmp[:], AX.X, ALU.add))
                link(dve.tensor_scalar(teid[:, 1:NT + 1], teid[:, 1:NT + 1], float(E - 1), None, ALU.min))
                dve.scalar_tensor_tensor(eid[:, g, :], teid[:, 0:NT + 1], float(E), teid[:, 1:NT + 2],
                                         ALU.mult, ALU.add)
                dve.wait_ge(s_ed, before(stage, ROUTES) + 1)
                link(dve.tensor_scalar(mx[0][:], ed[:, 0, :], 2.0, 2.0, ALU.mult, ALU.add))
                link(dve.reciprocal(mx[1][:], mx[0][:]))
                link(dve.tensor_scalar(wts[:, g, 0, :], mx[1][:], 1.0 / WS, None, ALU.mult))
                dve.tensor_tensor(wts[:, g, 1, :], wts[:, g, 0, :], ed[:, 0, :], ALU.mult).then_inc(s_routed, 1)

            def weights():
                dve.wait_ge(s_small, 16 * 3)
                dve.wait_ge(s_wexp, 1)
                dve.tensor_scalar(omix[:], vecs[:, 0:3], -1.0, 1.0, ALU.mult, ALU.add)
                link(dve.tensor_scalar(wdec[:, 0:1], wdec[:, 0:1], -1.0, None, ALU.mult))
                dve.tensor_tensor(wdec[:, 1:2], wdec[:, 0:1], vecs[:, 4:5], ALU.add)
                dve.tensor_scalar(wfull[:], wfull[:], wdec[:, 0:1], None, ALU.add)
                for i in range(3):
                    dve.tensor_scalar(qkv_f[:, i, :], att_raw[:, i, :], vecs[:, i:i + 1], None, ALU.mult)
                    ins = dve.tensor_scalar(qkv_f[:, 3 + i, :], att_raw[:, i, :], omix[:, i:i + 1], None, ALU.mult)
                ins.then_inc(s_qf, 1)
                with dve.Fori(0, E) as e:
                    for i in range(2):
                        dve.wait_ge(s_uphi, 2 * e + i + 1)
                        dve.scalar_tensor_tensor(
                            up_w[:, bass.ds(e, 1), 2 * i + 1, :].rearrange("p e f -> p (e f)"), stage_w[:, i, :], WS,
                            up_w[:, bass.ds(e, 1), 2 * i, :].rearrange("p e f -> p (e f)"),
                            ALU.mult, ALU.subtract).then_inc(s_uplo, 1)
                dve.wait_ge(s_qf, 1)
                dve.wait_ge(s_qhi, 1)
                dve.scalar_tensor_tensor(qkv_w[:, :, 1, :], qkv_f[:], WS, qkv_w[:, :, 0, :],
                                         ALU.mult, ALU.subtract).then_inc(s_qlo, 1)

            def ffn(stage):
                n0 = before(stage, TILES)

                def copy_T(t, k):
                    dve.wait_ge(s_turn, n0 + t + 3)
                    dve.wait_ge(s_up, 2 * (n0 + t) + 2)
                    dve.tensor_copy(rT[:, k, :, :], pT[:]).then_inc(s_rT, 1)

                def gate_half(t, k, q):
                    dve.wait_ge(s_sil, 2 * (n0 + t) + q + 1)
                    dve.wait_ge(s_y, n0 + t + 1)
                    dve.tensor_tensor(h[:, k, 2 * q:2 * q + 2, :], sil[:, q, :].rearrange("p (c t) -> p c t", c=2),
                                      pb[q][:].rearrange("p (c t) -> p c t", c=2), ALU.mult).then_inc(s_h, 1)

                def tile(t, k, i):
                    gate_half(t, k, 0)
                    if not (isinstance(t, int) and t == NT - 1):
                        copy_T(t + 1, 1 - k)
                    gate_half(t, k, 1)

                copy_T(0, 0)
                each_tile(dve, tile)

            def combine(stage, b):
                g, c0 = stage[1], before(stage, COMBINES) + b
                dve.wait_ge(s_gat[b % 2], 16 * TOPK * JU * (c0 // 2 + 1))
                for c in range(TOPK):
                    for j in range(JU):
                        jj = b * JU + j
                        ins = dve.scalar_tensor_tensor(xres[:, g * JG + jj, :], yg[:, b % 2, c, j, :],
                                                       wts[:, g, c, jj:jj + 1], xres[:, g * JG + jj, :],
                                                       ALU.mult, ALU.add)
                    if c == 0:
                        link(ins)
                ins.then_inc(s_comb, 1)
                dve.wait_ge(s_comb, c0 + 1)

            def mix(stage):
                g, m0 = stage[1], before(stage, MIXES)

                def take(b):
                    combine(stage, b)
                    normalise(stage, b)
                    parts_lo(stage, b)

                def wkv(b):
                    k, v, r = kk[:, b % 2, :], vv[:, b % 2, :], er[:, b % 2, :]
                    dve.wait_ge(s_bread, b_use(stage, f"k{b}"))
                    link(dve.tensor_tensor_scan(pp[:, 1:], wfull[:], k, NEG, ALU.add, ALU.max))
                    link(dve.scalar_tensor_tensor(dd[:], pp[:, 0:S], vecs[:, 4:5], k, ALU.subtract, ALU.subtract))
                    dve.tensor_scalar(mn[:, 0, :], dd[:], 0.0, None, ALU.min)
                    dve.tensor_scalar(mxx[:, 0, :], dd[:], 0.0, None, ALU.max)
                    dve.tensor_scalar(mn[:, 1, :], dd[:], wdec[:, 1:2], 0.0, ALU.add, ALU.min)
                    dve.tensor_scalar(mxx[:, 1, :], dd[:], wdec[:, 1:2], 0.0, ALU.add, ALU.max).then_inc(s_min, 1)
                    dve.wait_ge(s_exp, 2 * (m0 + b) + 2)
                    dve.wait_ge(s_aread, a_use(stage, f"v{b}"))
                    link(dve.tensor_tensor(kv[:], e2[:, 1, :], v, ALU.mult))
                    dve.tensor_tensor_scan(aa[:, 1:], e1[:, 1, :], kv[:], 0.0, ALU.mult, ALU.add)
                    link(dve.tensor_tensor_scan(bb[:, 1:], e1[:, 1, :], e2[:, 1, :], 0.0, ALU.mult, ALU.add))
                    dve.tensor_tensor(num[:], e1[:, 0, :], aa[:, 0:S], ALU.mult)
                    dve.tensor_tensor(tm[:], e2[:, 0, :], v, ALU.mult)
                    link(dve.tensor_tensor(den[:], e1[:, 0, :], bb[:, 0:S], ALU.mult))
                    dve.tensor_tensor(num[:], num[:], tm[:], ALU.add)
                    link(dve.tensor_tensor(den[:], den[:], e2[:, 0, :], ALU.add))
                    dve.wait_ge(s_bread, b_use(stage, f"r{b}"))
                    link(dve.scalar_tensor_tensor(den[:], r, 1.0, den[:], ALU.add, ALU.mult))
                    link(dve.reciprocal(tm[:], den[:]))
                    dve.tensor_tensor(att[:], num[:], tm[:], ALU.mult).then_inc(s_att, 1)

                def add(b):
                    j0 = (g * UG + b) * JU
                    dve.wait_ge(s_afull, a_use(stage, f"out{b}"))
                    link(dve.tensor_tensor(xres[:, j0:j0 + JU, :], xres[:, j0:j0 + JU, :],
                                           bkA[:].rearrange("p (j d) -> p j d", d=D), ALU.add))
                    dve.sem_inc(s_aread, 1)

                take(0)
                for b in range(UG):
                    if b >= 1:
                        add(b - 1)
                    if b + 1 < UG:
                        take(b + 1)
                    wkv(b)
                add(UG - 1)

            for stage in STAGES:
                if stage[0] == "route":
                    route(stage)
                if stage[0] == "ffn":
                    ffn(stage)
                if stage[0] == "mix":
                    mix(stage)
                if stage[0] == "last":
                    for b in range(UG):
                        combine(stage, b)
                if stage == STAGES[0]:
                    weights()

        @block.tensor
        def _(pe):
            pe.sem_inc(s_turn, 2)
            pe.sem_inc(s_up, 4)
            pe.sem_inc(s_y, 2)
            pe.wait_ge(s_const, 7)

            def bank_free(s_read, uses):
                if uses > 1:
                    pe.wait_ge(s_read, uses - 1)

            def route(stage):
                for b in range(UG):
                    u = before(stage, NORMS) + b
                    pe.wait_ge(s_xn, u + 1)
                    bank_free(s_aread, a_use(stage, f"turn{b}"))
                    for j in range(JU):
                        mm = pe.transpose(bkA[:, j * P:(j + 1) * P], xn[:, u % 2, j, :], ident[:])
                    mm.then_inc(s_afull, 1)
                    pe.wait_ge(s_small, 16 * 3)
                    pe.wait_ge(s_aread, a_use(stage, f"turn{b}"))
                    bank_free(s_bread, b_use(stage, f"logits{b}"))
                    for j in range(JU):
                        mm = pe.matmul(bkB[:, j * E:(j + 1) * E], xnT[:, j * P:(j + 1) * P], gate_w[:],
                                       start=True, stop=True)
                    mm.then_inc(s_bfull, 1)
                pe.wait_ge(s_chosen, before(stage, ROUTES) + 1)
                cv = chosen[:].rearrange("p j e -> p (j e)")
                bank_free(s_bread, b_use(stage, "totals"))
                pe.matmul(bkB[:, 0:JG * E], ones16[:], cv, start=True, stop=True).then_inc(s_bfull, 1)
                bank_free(s_aread, a_use(stage, "prefix"))
                pe.matmul(bkA[:, 0:JG * E], upper[:], cv, start=True, stop=True).then_inc(s_afull, 1)

            def ffn(stage):
                g, n0, run_no = stage[1], before(stage, TILES), before(stage, RUNS)

                def turn(t, k, m):
                    pe.wait_ge(s_rin[k], 16 * (SLOT_TILES[k] * run_no + m + 1))
                    pe.wait_ge(s_rT, n0 + t + 2)
                    for part in range(2):
                        for hh in range(TH):
                            mm = pe.transpose(pT[:, part, hh * P:(hh + 1) * P],
                                              rin[:, k, hh, part * D:(part + 1) * D], ident16[:])
                    mm.then_inc(s_turn, 1)

                up_bytes = up_w[:].rearrange("p e a f -> p (e a f)").bitcast(U8)
                down_bytes = down_w[:].rearrange("p e c d -> p (e c d)").bitcast(U8)

                def up_half(t, k, q, e):
                    pe.wait_ge(s_h, 2 * (n0 + t) + q + 1)
                    for c in range(2):
                        for bank, w in ((pa[q], 0), (pb[q], 2)):
                            for n, (wp, xp) in enumerate(((0, 0), (0, 1), (1, 0))):
                                at = 2 * ((w + wp) * F + (2 * q + c) * P)
                                mm = pe.matmul(bank[:, c * T:(c + 1) * T],
                                               up_bytes[:, bass.ds(e * (2 * 4 * F) + at, 2 * P)].bitcast(F16),
                                               rT[:, k, xp, :], start=(n == 0), stop=(n == 2))
                    mm.then_inc(s_up, 1)

                def experts(t):
                    both = pe.value_load(eid[0:1, g, bass.ds(t, 1)], min_val=0, max_val=E * E - 1)
                    return pe.snap(both % E, min_val=0, max_val=E - 1), pe.snap(both // E, min_val=0, max_val=E - 1)

                def down(t, k, e):
                    pe.wait_ge(s_h, 2 * (n0 + t) + 4)
                    pe.wait_ge(s_yrow, n0 + t + 2)
                    for c in range(FC):
                        rhs = down_bytes[:, bass.ds(e * (4 * FC * D) + 4 * c * D, 4 * D)].bitcast(F32)
                        for hh in range(TH):
                            mm = pe.matmul(py[:, hh, :], h[:, k, c, hh * P:(hh + 1) * P], rhs,
                                           start=(c == 0 and hh == 0), stop=(c == FC - 1), skip_group_check=True)
                    mm.then_inc(s_y, 1)

                def tile(t, k, i):
                    cur, prev = experts(t)
                    pe.wait_ge(s_rT, n0 + t + 3)
                    up_half(t, k, 0, cur)
                    if not (isinstance(t, int) and t == NT - 1):
                        turn(t + 1, 1 - k, 0 if i is None else i + 1)
                    up_half(t, k, 1, cur)
                    if i is not None:
                        down(t - 1, 1 - k, prev)

                if run_no == 0:
                    pe.wait_ge(s_uplo, 2 * E + 2)
                    pe.wait_ge(s_w2, 16)
                pe.wait_ge(s_routed, before(("route", g, stage[2]), ROUTES) + 1)
                turn(0, 0, 0)
                each_tile(pe, tile)
                down(NT - 1, 0, experts(NT)[1])

            def mix(stage):
                g, m0 = stage[1], before(stage, MIXES)

                def turn(b):
                    pe.wait_ge(s_lo, before(stage, NORMS) + b + 1)
                    bank_free(s_aread, a_use(stage, f"turn{b}"))
                    a16 = bkA[:].bitcast(F16)
                    for part in range(2):
                        for j in range(JU):
                            mm = pe.transpose(a16[:, part * S + j * P:part * S + (j + 1) * P],
                                              parts[:, g, b * JU + j, part * D:(part + 1) * D], ident16[:])
                    mm.then_inc(s_afull, 1)

                def project(b, i, bank):
                    n = 0
                    for f, start in ((i, 2), (3 + i, 1)):
                        for wp, xp in ((0, 0), (0, 1), (1, 0)):
                            mm = pe.matmul(bank[:], qkv_w[:, f, wp, :], xT[:, b % 2, xp, start:start + S],
                                           start=(n == 0), stop=(n == 5))
                            n += 1
                    return mm

                def out_proj(b):
                    pe.wait_ge(s_att, m0 + b + 1)
                    bank_free(s_aread, a_use(stage, f"out{b}"))
                    for j in range(JU):
                        mm = pe.matmul(bkA[:, j * P:(j + 1) * P], att[:, j * P:(j + 1) * P], att_raw[:, 3, :],
                                       start=True, stop=True)
                    mm.then_inc(s_afull, 1)

                pe.wait_ge(s_qlo, 1)
                turn(0)
                for b in range(UG):
                    pe.wait_ge(s_aread, a_use(stage, f"turn{b}"))
                    bank_free(s_bread, b_use(stage, f"k{b}"))
                    project(b, 0, bkB).then_inc(s_bfull, 1)
                    bank_free(s_aread, a_use(stage, f"v{b}"))
                    project(b, 1, bkA).then_inc(s_afull, 1)
                    bank_free(s_bread, b_use(stage, f"r{b}"))
                    project(b, 2, bkB).then_inc(s_bfull, 1)
                    if b + 1 < UG:
                        turn(b + 1)
                    out_proj(b)

            for stage in STAGES:
                if stage[0] == "route":
                    route(stage)
                if stage[0] == "ffn":
                    ffn(stage)
                if stage[0] == "mix":
                    mix(stage)


def kernel(L0_attn_x, L0_attn_time_mix_k, L0_attn_time_mix_v, L0_attn_time_mix_r, L0_attn_time_decay,
           L0_attn_time_first, L0_attn_Wk, L0_attn_Wv, L0_attn_Wr, L0_attn_Wo, L0_ffn_gate_w, L0_ffn_w1,
           L0_ffn_w3, L0_ffn_w2):
    import numpy as np
    import concourse.bacc as bacc
    from concourse.bass_utils import run_bass_kernel_spmd

    vec = [L0_attn_time_mix_k, L0_attn_time_mix_v, L0_attn_time_mix_r, L0_attn_time_decay, L0_attn_time_first]
    arrays = {
        "x": np.ascontiguousarray(L0_attn_x),
        "channel_vecs": np.ascontiguousarray(np.stack([np.asarray(v).reshape(D) for v in vec], axis=1)),
        "att_w": np.ascontiguousarray(np.stack(
            [np.asarray(w).T for w in (L0_attn_Wk, L0_attn_Wv, L0_attn_Wr, L0_attn_Wo)], axis=1)),
        "gate": np.ascontiguousarray(L0_ffn_gate_w),
        "w1": np.ascontiguousarray(L0_ffn_w1),
        "w3": np.ascontiguousarray(L0_ffn_w3),
        "w2": np.ascontiguousarray(L0_ffn_w2),
    }
    nc = bacc.Bacc("TRN2", target_bir_lowering=False, num_devices=1)
    args = [nc.dram_tensor(f"in_{n}", a.shape, mybir.dt.from_np(a.dtype), kind="ExternalInput").ap()
            for n, a in arrays.items()]
    out = nc.dram_tensor("out_0", (B, S, D), F32, kind="ExternalOutput").ap()
    macaron_kernel(nc, *args, out)
    r = run_bass_kernel_spmd(nc, [{f"in_{n}": a for n, a in arrays.items()}], core_ids=[0])
    return r.results[0]["out_0"]
```

```python
from contextlib import ExitStack

import concourse.bass as bass
from concourse import mybir

ALU = mybir.AluOpType
ACT = mybir.ActivationFunctionType
AX = mybir.AxisListType
F32 = mybir.dt.float32
F16 = mybir.dt.float16
BF16 = mybir.dt.bfloat16
I32 = mybir.dt.int32
U8 = mybir.dt.uint8

P = 128
B, S, D = 8, 512, 128
E, F, TOPK = 8, 512, 2
FC = F // P
JU = S // P
UNITS = (3, 3, 2)
GROUPS = len(UNITS)
U0 = tuple(sum(UNITS[:g]) for g in range(GROUPS))
UG = max(UNITS)
JG = UG * JU
T = 256
TH = T // P
NT = tuple((u * S * TOPK + E * (T - 1)) // T for u in UNITS)
RUNS = 2 * GROUPS
START = tuple(sum(NT[q % GROUPS] for q in range(r)) for r in range(RUNS + 1))
TILES = START[RUNS]
HALVES = 2 * TILES
EPS = 1e-5
WS = 64.0
MAGIC = 0x5F3759DF
NEG = -1e30
BIG = 3e38

WRING = 2
SLOTS = 2
RING = 2 * SLOTS
LOOPED = 148

NORM = [("stats", 0), ("norm", 1), ("hi", 2), ("lo", 3), ("turn", 3), ("xnT", 4), ("logits", 5), ("keep", 6)]
MIX = [("combine", 0), ("mstats", 1), ("mnorm", 2), ("hi_m", 3), ("lo_m", 4), ("turn_m", 5), ("xT", 6), ("pk", 7),
       ("k", 8), ("pv", 8), ("v", 9), ("pr", 9), ("peak", 9), ("gaps", 10), ("r", 11), ("exps", 11), ("exps2", 12),
       ("sum_a", 13), ("sum_b", 14), ("weigh", 15), ("total", 16), ("divide", 17), ("divide2", 18), ("att", 19),
       ("out", 20), ("add", 21)]
CHOOSE = [("pick", 0), ("pick2", 1), ("count", 2), ("place", 3), ("scatter", 4), ("tiles", 4)]


APART = (9, 9, 9)

HOLDS = [("turn", "A", "xnT"), ("turn_m", "A", "xT"), ("pv", "A", "v"), ("out", "A", "add"), ("count", "A", "place"),
         ("logits", "B", "keep"), ("pk", "B", "k"), ("pr", "B", "r"), ("count", "B", "place"),
         ("stats", "stats", "hi"), ("mstats", "stats", "hi_m"),
         ("norm", "xn", "lo"), ("mnorm", "xn", "lo_m"), ("xnT", "xnT", "keep"), ("pick", "routing", "tiles"),
         ("peak", "gaps", "exps2"), ("exps", "exps", "total"), ("sum_a", "sums", "att")]


def make_plan():
    plan, taken = [], set()

    def put(steps, start, run, b):
        at = dict(steps)
        while True:
            holds = {(what, start + i) for step, what, until in HOLDS if step in at
                     for i in range(at[step], at[until])}
            if not holds & taken:
                break
            start += 1
        taken.update(holds)
        plan.extend((start + i, step, run, b) for step, i in steps)
        return start

    def route(run, starts, last_placed):
        for b, start in enumerate(starts):
            at = put(NORM, max(start, last_placed - 5), run, b)
        return put(CHOOSE, at + len(NORM), run, 0) + dict(CHOOSE)["place"]

    placed = -100
    for run in range(GROUPS):
        placed = route(run, [max(placed, -100 if run == 0 else 0) + 2 * b for b in range(UNITS[run])], placed)
        placed = max(placed, 0)
    free = 0
    for g in range(GROUPS):
        stored = 2 * START[g + 1] + 2
        starts = []
        for b in range(UNITS[g]):
            plan.append((stored, "gather", g, b))
            starts.append(put(MIX, max(stored + 3 + 4 * b, free), g, b))
            free = starts[-1] + APART[g]
        placed = route(GROUPS + g, [start + 22 for start in starts], placed)
    for g in range(GROUPS - 1):
        stored = 2 * START[GROUPS + g + 1] + 2
        for b in range(UNITS[g]):
            plan.append((stored, "gather", GROUPS + g, b))
            put([("combine", 0), ("write", 3)], stored + 3 + 4 * b, GROUPS + g, b)
    plan.sort(key=lambda p: (p[0], p[1] not in [until for _, _, until in HOLDS]))
    last = [(HALVES, step, RUNS - 1, b) for step in ("gather", "combine", "write") for b in range(UNITS[-1])]
    return plan + last


PLAN = make_plan()


def count(steps, upto):
    order = [p[1:] for p in PLAN if p[1] in steps]
    return order.index(upto) + 1


def wait(eng, sem, value):
    if not isinstance(value, int) or value > 0:
        eng.wait_ge(sem, value)


def in_order(eng, half, step, halves, before_halves=None):
    for _, name, run, b in (p for p in PLAN if p[0] < 0):
        step(name, run, b)
    if before_halves:
        before_halves()
    for n in range(LOOPED):
        half(n, n % RING)
        for _, name, run, b in (p for p in PLAN if p[0] == n):
            step(name, run, b)
    at = LOOPED
    stops = sorted({-(-p[0] // RING) * RING for p in PLAN if LOOPED <= p[0] < HALVES} | {halves})
    for stop in stops:
        if stop > at:
            with eng.Fori(at // RING, stop // RING) as i:
                for k in range(RING):
                    half(i * RING + k, k)
            at = stop
        for _, name, run, b in (p for p in PLAN if LOOPED <= p[0] < HALVES and -(-p[0] // RING) * RING == stop):
            step(name, run, b)


def last_steps(step):
    for _, name, run, b in (p for p in PLAN if p[0] == HALVES):
        step(name, run, b)


def macaron_kernel(nc, x, channel_vecs, att_w, gate, w1, w3, w2, out):
    with ExitStack() as ctx:
        def sb(name, shape, dt=F32):
            return ctx.enter_context(nc.sbuf_tensor(name, shape, dt))

        def ps(name, shape, dt=F32):
            return ctx.enter_context(nc.psum_tensor(name, shape, dt))

        def sem(name):
            return ctx.enter_context(nc.semaphore(name))

        rows_in = [nc.dram_tensor(f"rows_in{g}", (NT[g] * T, 2 * D), F16, kind="Internal").ap() for g in range(GROUPS)]
        rows_out = [nc.dram_tensor(f"rows_out{g}", (NT[g] * T, D), F32, kind="Internal").ap() for g in range(GROUPS)]

        xres = sb("xres", [P, B * JU, D])
        up_w = sb("up_w", [P, E, 4, F], F16)
        down_w = sb("down_w", [P, E, FC, D])
        stage_w = sb("stage_w", [P, 2, WRING, F])
        gate_w = sb("gate_w", [P, E])
        att_raw = sb("att_raw", [P, 4, D])
        qkv_f = sb("qkv_f", [P, 6, D])
        qkv_w = sb("qkv_w", [P, 6, 2, D], F16)
        vecs = sb("vecs", [P, 5])
        omix = sb("omix", [P, 3])
        wdec = sb("wdec", [P, 2])
        wfull = sb("wfull", [P, S])
        ident = sb("ident", [P, P])
        ident16 = sb("ident16", [P, P], F16)
        upper = sb("upper", [P, P], BF16)
        ones16 = sb("ones16", [P, P], BF16)
        zrow = sb("zrow", [P, 2 * D], F16)
        e_desc = sb("e_desc", [P, JG, E])
        t_iota = sb("t_iota", [P, max(NT), E])
        stats = sb("stats", [P, JU, 6])
        mv = sb("mv", [P, JU, 2])
        var = sb("var", [P, JU])
        bits = sb("bits", [P, JU], I32)
        rstd = sb("rstd", [P, JU])
        nwt = sb("nwt", [P, JU])
        xn = sb("xn", [P, 2, JU, D])
        parts = sb("parts", [P, B * JU, 2 * D], F16)
        xnT = sb("xnT", [P, S])
        logit = sb("logit", [P, JG, E])
        rt = [sb(f"rt{i}", [P, JG, E]) for i in range(3)]
        pick = [sb(f"pick{i}", [P, JG, E]) for i in range(2)]
        mx = [sb(f"mx{i}", [P, JG]) for i in range(2)]
        kx = sb("kx", [P, JG])
        chosen = sb("chosen", [P, JG, E], BF16)
        cnt = sb("cnt", [P, E * JG])
        run_s = sb("run_s", [P, E * JG])
        one_s = sb("one_s", [P, E * JG])
        ne = sb("ne", [P, 6, E])
        nei = sb("nei", [P, E], I32)
        tcmp = sb("tcmp", [P, max(NT), E])
        teid = sb("teid", [P, TILES + 1])
        slotf = sb("slotf", [P, 2, JG])
        slot = sb("slot", [P, 2, B * JU], I32)
        wts = sb("wts", [P, 2, B * JU])
        ed = sb("ed", [P, 2, JG])
        eid = sb("eid", [P, TILES], I32)
        rin = sb("rin", [P, SLOTS, TH, 2 * D], F16)
        rT = sb("rT", [P, SLOTS, 2, T], F16)
        sil = sb("sil", [P, 2, FC // 2 * T])
        h = sb("h", [P, RING, FC // 2, T])
        yrow = sb("yrow", [P, SLOTS, TH, D])
        yg = sb("yg", [P, UG, TOPK, JU, D])
        xT = sb("xT", [P, 2, 2, S + 2], F16)
        kk = sb("kk", [P, 2, S])
        vv = sb("vv", [P, 2, S])
        er = sb("er", [P, 2, S])
        pp = sb("pp", [P, S + 1])
        dd = sb("dd", [P, S])
        mn = sb("mn", [P, 2, S])
        mxx = sb("mxx", [P, 2, S])
        e1 = sb("e1", [P, 2, S])
        e2 = sb("e2", [P, 2, S])
        kv = sb("kv", [P, S])
        aa = sb("aa", [P, S + 1])
        bb = sb("bb", [P, S + 1])
        num = sb("num", [P, S])
        den = sb("den", [P, S])
        tm = sb("tm", [P, S])
        att = sb("att", [P, S])

        pa = [ps(f"pa{q}", [P, FC // 2 * T]) for q in range(2)]
        pb = [ps(f"pb{q}", [P, FC // 2 * T]) for q in range(2)]
        pT = ps("pT", [P, 2, T], F16)
        py = ps("py", [P, TH, D])
        bkA = ps("bkA", [P, S])
        bkB = ps("bkB", [P, S])

        s_x = [sem(f"x_in{g}") for g in range(GROUPS)]
        s_small = sem("small_in")
        s_stage = [sem(f"stage_in{i}") for i in range(WRING)]
        s_w2 = sem("w2_in")
        s_zrow = sem("zrow_made")
        s_fill = [sem(f"rows_zeroed{g}") for g in range(GROUPS)]
        s_const = sem("const_made")
        s_uphi = sem("up_hi_made")
        s_uplo = sem("up_lo_made")
        s_qf = sem("qkv_folded")
        s_qhi = sem("qkv_hi_made")
        s_qlo = sem("qkv_lo_made")
        s_wexp = sem("decay_exp_made")
        s_chain = sem("dve_chain")
        s_xn = sem("xn_made")
        s_hi = sem("parts_hi_made")
        s_lo = sem("parts_lo_made")
        s_afull = sem("bankA_full")
        s_aread = sem("bankA_read")
        s_bfull = sem("bankB_full")
        s_bread = sem("bankB_read")
        s_chosen = sem("chosen_made")
        s_ed = sem("gap_exp_made")
        s_slots = sem("slots_made")
        s_routed = sem("routed")
        s_scat = [sem(f"scattered{g}") for g in range(GROUPS)]
        s_rin = [sem(f"tile_in{i}") for i in range(SLOTS)]
        s_turn = sem("tile_turned")
        s_rT = sem("tile_copied")
        s_up = sem("up_done")
        s_sil = sem("silu_done")
        s_h = sem("h_made")
        s_y = sem("down_done")
        s_yrow = sem("y_copied")
        s_yst = [sem(f"y_stored{i}") for i in range(SLOTS)]
        s_gat = [sem(f"gathered{b}") for b in range(UG)]
        s_comb = sem("combined")
        s_min = sem("minmax_made")
        s_exp = sem("exps_made")
        s_sums = sem("sums_made")
        s_att = sem("att_made")
        s_out = sem("out_stored")

        block = ctx.enter_context(nc.Block())

        A_STEPS = ("turn", "turn_m", "pv", "out", "count")
        B_STEPS = ("logits", "pk", "pr", "count")
        NORMS = ("norm", "mnorm")
        SPLITS = {"norm": "hi", "mnorm": "hi_m"}

        def units(run, b):
            u = U0[run % GROUPS] + b
            return u, slice(u * JU, (u + 1) * JU)

        def tile_of(n, k):
            return (n - k) // 2 + k // 2, k // 2

        def xn_slot(name, run, b):
            return (count(NORMS, (name, run, b)) - 1) % 2

        @block.sync
        def _(sp):
            xv = x.rearrange("b (j p) d -> p (b j) d", p=P)
            ov = out.rearrange("b (j p) d -> p (b j) d", p=P)
            for u in range(UNITS[0]):
                sp.dma_start(xres[:, u * JU:(u + 1) * JU, :], xv[:, u * JU:(u + 1) * JU, :]).then_inc(s_x[0], 16)
            sp.dma_start(gate_w[:], gate).then_inc(s_small, 16)
            sp.dma_start(vecs[:], channel_vecs).then_inc(s_small, 16)
            sp.dma_start(att_raw[:], att_w).then_inc(s_small, 16)

            def fill(g):
                sp.dma_start(rows_in[g].rearrange("(p r) c -> p r c", p=P),
                             zrow[:, None, :].to_broadcast([P, NT[g] * TH, 2 * D])).then_inc(s_fill[g], 16)

            sp.wait_ge(s_zrow, 1)
            fill(0)
            with sp.Fori(0, E // WRING) as i:
                for k in range(WRING):
                    sp.wait_ge(s_uplo, i * WRING + k + 1)
                    for n, a in enumerate((w1, w3)):
                        sp.dma_start(stage_w[:, n, k, :], a[bass.ds(i * WRING + k, 1), :, :].rearrange(
                            "e d f -> d (e f)")).then_inc(s_stage[k], 16)
            sp.dma_start(down_w[:], w2.rearrange("e (c p) d -> p e c d", p=P)).then_inc(s_w2, 16)
            for g in range(1, GROUPS):
                js = slice(U0[g] * JU, (U0[g] + UNITS[g]) * JU)
                sp.dma_start(xres[:, js, :], xv[:, js, :]).then_inc(s_x[g], 16)
                fill(g)

            def rows(tensors, t):
                run = max(r for r in range(RUNS) if START[r] <= t)
                i = t - START[run]
                return tensors[run % GROUPS][i * T:(i + 1) * T, :].rearrange("(h p) c -> p h c", p=P)

            def load(t):
                if t in START:
                    run = START.index(t)
                    sp.wait_ge(s_scat[run % GROUPS], 16 * TOPK * JU * UNITS[run % GROUPS] * (run // GROUPS + 1))
                wait(sp, s_turn, t - SLOTS + 1)
                sp.dma_start(rin[:, t % SLOTS, :, :], rows(rows_in, t)).then_inc(s_rin[t % SLOTS], 16)

            def store(t):
                sp.wait_ge(s_yrow, t + 1)
                sp.dma_start(rows(rows_out, t), yrow[:, t % SLOTS, :, :]).then_inc(s_yst[t % SLOTS], 16)

            def step(name, run, b):
                if name == "write":
                    u, js = units(run, b)
                    sp.wait_ge(s_comb, count(("combine",), ("combine", run, b)))
                    sp.dma_start(ov[:, js, :], xres[:, js, :]).then_inc(s_out, 16)

            for t in range(SLOTS):
                load(t)
            for t in range(TILES + 1):
                if t + SLOTS < TILES:
                    load(t + SLOTS)
                if t >= 1:
                    store(t - 1)
                for _, name, run, b in (p for p in PLAN if p[0] in (2 * t, 2 * t + 1)):
                    step(name, run, b)
            sp.wait_ge(s_out, 16 * B)

        @block.gpsimd
        def _(pool):
            pool.memset(ident[:], 0.0).then_inc(s_const, 1)
            pool.memset(upper[:], 0.0).then_inc(s_const, 1)
            pool.wait_ge(s_const, 2)
            pool.affine_select(out=ident[:], in_=ident[:], compare_op=ALU.not_equal, fill=1.0, base=0,
                               pattern=[[-1, P]], channel_multiplier=1).then_inc(s_const, 1)
            pool.affine_select(out=upper[:], in_=upper[:], compare_op=ALU.is_ge, fill=1.0, base=0,
                               pattern=[[-1, P]], channel_multiplier=1).then_inc(s_const, 1)
            pool.wait_ge(s_const, 4)
            pool.tensor_copy(ident16[:], ident[:]).then_inc(s_const, 1)
            pool.iota(e_desc[:], [[0, JG], [-1, E]], E, 0, allow_small_or_imprecise_dtypes=True).then_inc(s_const, 1)
            pool.iota(t_iota[:], [[1, max(NT)], [0, E]], 0, 0, allow_small_or_imprecise_dtypes=True).then_inc(s_const, 1)

            for _, name, run, b in PLAN:
                g = run % GROUPS
                if name == "scatter":
                    pool.wait_ge(s_slots, run + 1)
                    pool.wait_ge(s_lo, max(count(("lo", "lo_m"), ("lo", run, i)) for i in range(UNITS[g])))
                    if run < GROUPS:
                        pool.wait_ge(s_fill[g], 16)
                    for j in range(U0[g] * JU, (U0[g] + UNITS[g]) * JU):
                        for c in range(TOPK):
                            pool.indirect_dma_start(
                                rows_in[g][:], bass.IndirectOffsetOnAxis(ap=slot[:, c, j:j + 1], axis=0),
                                parts[:, j, :], None).then_inc(s_scat[g], 16)
                if name == "gather":
                    if b == 0:
                        for k in range(SLOTS):
                            pool.wait_ge(s_yst[k], 16 * len(range(k, START[run + 1], SLOTS)))
                    before = [p[1:] for p in PLAN if p[1] == "gather" and p[3] == b]
                    if before.index((name, run, b)):
                        _, last_run, _ = before[before.index((name, run, b)) - 1]
                        pool.wait_ge(s_comb, count(("combine",), ("combine", last_run, b)))
                    for j in range(JU):
                        for c in range(TOPK):
                            pool.indirect_dma_start(
                                yg[:, b, c, j, :], None, rows_out[g][:],
                                bass.IndirectOffsetOnAxis(ap=slot[:, c, (U0[g] + b) * JU + j:(U0[g] + b) * JU + j + 1], axis=0)
                            ).then_inc(s_gat[b], 16)

        @block.scalar
        def _(act):
            act.wait_ge(s_small, 16 * 3)
            act.activation(wdec[:, 0:1], vecs[:, 3:4], ACT.Exp).then_inc(s_wexp, 1)

            def split_weights():
                with act.Fori(0, E // WRING) as i:
                    for k in range(WRING):
                        act.wait_ge(s_stage[k], 32 * i + 32)
                        act.activation(up_w[:, bass.ds(i * WRING + k, 1), 0::2, :].rearrange("p e a f -> p (e a) f"),
                                       stage_w[:, :, k, :], ACT.Copy, scale=WS).then_inc(s_uphi, 1)
                act.wait_ge(s_qf, 1)
                act.activation(qkv_w[:, :, 0, :], qkv_f[:], ACT.Copy, scale=WS).then_inc(s_qhi, 1)

            def copy_T(t, slot, halves_done=0):
                act.wait_ge(s_turn, t + 1)
                wait(act, s_up, halves_done)
                act.activation(rT[:, slot, :, :], pT[:], ACT.Copy).then_inc(s_rT, 1)

            def copy_y(t, slot, rounds):
                act.wait_ge(s_y, 2 * t + 2)
                wait(act, s_yst[slot], 16 * rounds)
                act.activation(yrow[:, slot, :, :], py[:], ACT.Copy).then_inc(s_yrow, 1)

            def half(n, k):
                t, slot = tile_of(n, k)
                if k % 2 == 0 and not (isinstance(n, int) and n == HALVES - 2):
                    copy_T(t + 1, (slot + 1) % SLOTS, n)
                act.wait_ge(s_up, n + 1)
                act.activation(sil[:, k % 2, :], pa[k % 2][:], ACT.Silu, scale=1.0 / WS).then_inc(s_sil, 1)
                if k % 2 and not (isinstance(n, int) and n == 1):
                    copy_y(t - 1, (slot - 1) % SLOTS, (n - k - (RING if k == 1 else 0)) // RING)

            def step(name, run, b):
                u, js = units(run, b)
                me = (name, run, b)
                if name in ("hi", "hi_m"):
                    src = ("norm" if name == "hi" else "mnorm", run, b)
                    act.wait_ge(s_xn, count(NORMS, src))
                    act.activation(parts[:, js, 0:D], xn[:, xn_slot(*src), :, :], ACT.Copy).then_inc(s_hi, 1)
                if name == "xnT":
                    act.wait_ge(s_afull, count(A_STEPS, ("turn", run, b)))
                    wait(act, s_bfull, count(("xnT",), me) and last_logits(run, b))
                    act.activation(xnT[:], bkA[:], ACT.Copy).then_inc(s_aread, 1)
                if name == "keep":
                    act.wait_ge(s_bfull, count(B_STEPS, ("logits", run, b)))
                    wait(act, s_chosen, run)
                    act.activation(logit[:, b * JU:(b + 1) * JU, :],
                                   bkB[:, 0:JU * E].rearrange("p (j e) -> p j e", e=E), ACT.Copy).then_inc(s_bread, 1)
                if name == "count":
                    act.wait_ge(s_chosen, run + 1)
                    jg = JU * UNITS[run % GROUPS]
                    act.activation(ed[:, 0, 0:jg], ed[:, 1, 0:jg], ACT.Exp).then_inc(s_ed, 1)
                if name == "xT":
                    act.wait_ge(s_afull, count(A_STEPS, ("turn_m", run, b)))
                    act.activation(xT[:, u % 2, :, 2:S + 2], bkA[:].bitcast(F16).rearrange("p (h s) -> p h s", h=2),
                                   ACT.Copy).then_inc(s_aread, 1)
                if name == "k":
                    act.wait_ge(s_bfull, count(B_STEPS, ("pk", run, b)))
                    wait(act, s_att, count(("att",), ("att", run, b)) - 2)
                    act.activation(kk[:, u % 2, :], bkB[:], ACT.Copy, scale=1.0 / WS).then_inc(s_bread, 1)
                if name == "v":
                    act.wait_ge(s_afull, count(A_STEPS, ("pv", run, b)))
                    act.activation(vv[:, u % 2, :], bkA[:], ACT.Copy, scale=1.0 / WS).then_inc(s_aread, 1)
                if name == "r":
                    act.wait_ge(s_bfull, count(B_STEPS, ("pr", run, b)))
                    act.activation(er[:, u % 2, :], bkB[:], ACT.Exp, scale=-1.0 / WS).then_inc(s_bread, 1)
                if name == "exps":
                    act.wait_ge(s_min, count(("gaps",), ("gaps", run, b)))
                    wait(act, s_sums, count(("total",), ("total", run, b)) - 1)
                    act.activation(e1[:], mn[:], ACT.Exp)
                if name == "exps2":
                    act.activation(e2[:], mxx[:], ACT.Exp, scale=-1.0).then_inc(s_exp, 1)

            def last_logits(run, b):
                i = count(("logits",), ("logits", run, b))
                order = [p[1:] for p in PLAN if p[1] == "logits"]
                return count(B_STEPS, order[i - 2]) if i >= 2 else 0

            in_order(act, half, step, before_halves=lambda: (split_weights(), copy_T(0, 0)), halves=HALVES - RING)
            for n in range(HALVES - RING, HALVES):
                half(n, n % RING)
            copy_y(TILES - 1, (TILES - 1) % SLOTS, (TILES - 1) // SLOTS)

        @block.vector
        def _(dve):
            chained = [0]

            def link(ins):
                chained[0] += 1
                ins.then_inc(s_chain, 1)
                dve.wait_ge(s_chain, chained[0])

            dve.memset(zrow[:], 0.0).then_inc(s_zrow, 1)
            dve.sem_inc(s_uplo, WRING)
            dve.memset(ones16[:], 1.0)
            dve.memset(one_s[:], 1.0)
            dve.memset(pp[:, 0:1], NEG)
            dve.memset(aa[:, 0:1], 0.0)
            dve.memset(bb[:, 0:1], 0.0)
            dve.memset(wfull[:], 0.0)
            dve.memset(teid[:], 0.0)
            link(dve.memset(xT[:, :, :, 0:2], 0.0))

            def statistics(run, b):
                _, js = units(run, b)
                for j in range(JU):
                    ins = dve.bn_stats(stats[:, j, :], xres[:, js, :][:, j, :])
                link(ins)
                for j in range(JU):
                    ins = dve.bn_aggr(mv[:, j, :], stats[:, j, :])
                link(ins)

            def normalise(name, run, b):
                _, js = units(run, b)
                i, at = count(NORMS, (name, run, b)), xn_slot(name, run, b)
                link(dve.tensor_scalar(var[:], mv[:, :, 1], EPS, None, ALU.add))
                link(dve.tensor_scalar(bits[:], var[:].bitcast(I32), 1, None, ALU.logical_shift_right))
                link(dve.tensor_scalar(rstd[:].bitcast(I32), bits[:], -1.0, float(MAGIC), ALU.mult, ALU.add))
                for _ in range(3):
                    link(dve.tensor_tensor(nwt[:], rstd[:], rstd[:], ALU.mult))
                    link(dve.scalar_tensor_tensor(nwt[:], nwt[:], -0.5, var[:], ALU.mult, ALU.mult))
                    link(dve.scalar_tensor_tensor(rstd[:], nwt[:], 1.5, rstd[:], ALU.add, ALU.mult))
                if i > 2:
                    order = [p[1:] for p in PLAN if p[1] in NORMS]
                    old, orun, ob = order[i - 3]
                    dve.wait_ge(s_hi, count(("hi", "hi_m"), (SPLITS[old], orun, ob)))
                    if old == "norm":
                        dve.wait_ge(s_afull, count(A_STEPS, ("turn", orun, ob)))
                for j in range(JU):
                    ins = dve.tensor_scalar(xn[:, at, j, :], xres[:, js, :][:, j, :], mv[:, j, 0:1], rstd[:, j:j + 1],
                                            ALU.subtract, ALU.mult)
                ins.then_inc(s_xn, 1)

            def parts_lo(name, run, b):
                u, js = units(run, b)
                src = ("norm" if name == "lo" else "mnorm", run, b)
                dve.wait_ge(s_xn, count(NORMS, src))
                dve.wait_ge(s_hi, count(("hi", "hi_m"), (SPLITS[src[0]], run, b)))
                dve.tensor_tensor(parts[:, js, D:2 * D], xn[:, xn_slot(*src), :, :], parts[:, js, 0:D],
                                  ALU.subtract).then_inc(s_lo, 1)

            def pick_expert(run, c):
                g = run % GROUPS
                jg = JU * UNITS[g]
                lg, masked, first, picked = logit[:, 0:jg, :], rt[0][:, 0:jg, :], rt[1][:, 0:jg, :], pick[c][:, 0:jg, :]

                def per_token(v):
                    return v[:, 0:jg, None].to_broadcast([P, jg, E])

                if c == 0:
                    dve.wait_ge(s_const, 7)
                    dve.wait_ge(s_bread, max(count(B_STEPS, ("logits", run, b)) for b in range(UNITS[g])))
                src = masked if c else lg
                link(dve.tensor_reduce(mx[c][:, 0:jg], src, AX.X, ALU.max))
                link(dve.tensor_tensor(first, src, per_token(mx[c]), ALU.is_equal))
                link(dve.tensor_tensor(first, first, e_desc[:, 0:jg, :], ALU.mult))
                link(dve.tensor_reduce(kx[:, 0:jg], first, AX.X, ALU.max))
                link(dve.tensor_tensor(picked, e_desc[:, 0:jg, :], per_token(kx), ALU.is_equal))
                if c == 0:
                    link(dve.scalar_tensor_tensor(masked, picked, -BIG, lg, ALU.mult, ALU.add))
                else:
                    wait(dve, s_ed, run)
                    dve.tensor_tensor(ed[:, 1, 0:jg], mx[1][:, 0:jg], mx[0][:, 0:jg], ALU.subtract)
                    dve.tensor_tensor(chosen[:, 0:jg, :], pick[0][:, 0:jg, :], pick[1][:, 0:jg, :],
                                      ALU.add).then_inc(s_chosen, 1)

            def place(run):
                g = run % GROUPS
                jg = JU * UNITS[g]
                js = slice(U0[g] * JU, U0[g] * JU + jg)
                cnt_f, run_f = cnt[:, 0:E * jg], run_s[:, 0:E * jg]
                cnt_e, run_e = (v.rearrange("p (e j) -> p e j", e=E) for v in (cnt_f, run_f))
                dve.wait_ge(s_bfull, count(B_STEPS, ("count", run, 0)))
                dve.tensor_copy(cnt_e, bkB[:, 0:jg * E].rearrange("p (j e) -> p e j", e=E)).then_inc(s_bread, 1)
                dve.wait_ge(s_bread, count(B_STEPS, ("count", run, 0)))
                link(dve.tensor_tensor_scan(run_f, one_s[:, 0:E * jg], cnt_f, 0.0, ALU.mult, ALU.add))
                link(dve.tensor_reduce(ne[:, 0, :], cnt_e, AX.X, ALU.add))
                link(dve.tensor_scalar(nei[:], ne[:, 0, :], float(T - 1), None, ALU.add))
                link(dve.tensor_scalar(nei[:], nei[:], T.bit_length() - 1, None, ALU.logical_shift_right))
                link(dve.tensor_copy(ne[:, 1, :], nei[:]))
                link(dve.tensor_tensor_scan(ne[:, 2, :], one_s[:, 0:E], ne[:, 1, :], 0.0, ALU.mult, ALU.add))
                link(dve.tensor_tensor(ne[:, 3, :], ne[:, 2, :], ne[:, 1, :], ALU.subtract))
                link(dve.tensor_tensor(ne[:, 4, :], run_e[:, :, jg - 1], ne[:, 0, :], ALU.subtract))
                link(dve.scalar_tensor_tensor(ne[:, 5, :], ne[:, 3, :], float(T), ne[:, 4, :], ALU.mult, ALU.subtract))
                link(dve.tensor_tensor(run_f, run_f, cnt_f, ALU.subtract))
                link(dve.tensor_tensor(run_e, run_e, ne[:, 5, :, None].to_broadcast([P, E, jg]), ALU.add))
                dve.wait_ge(s_afull, count(A_STEPS, ("count", run, 0)))
                dve.tensor_tensor(rt[0][:, 0:jg, :], bkA[:, 0:jg * E].rearrange("p (j e) -> p j e", e=E),
                                  run_e.rearrange("p e j -> p j e"), ALU.add).then_inc(s_aread, 1)
                dve.wait_ge(s_aread, count(A_STEPS, ("count", run, 0)))
                for c in range(TOPK):
                    link(dve.tensor_tensor(rt[1 + c][:, 0:jg, :], rt[0][:, 0:jg, :], pick[c][:, 0:jg, :], ALU.mult))
                for c in range(TOPK):
                    link(dve.tensor_reduce(slotf[:, c, 0:jg], rt[1 + c][:, 0:jg, :], AX.X, ALU.add))
                dve.tensor_copy(slot[:, :, js], slotf[:, :, 0:jg]).then_inc(s_slots, 1)

            def tiles_and_weights(run):
                g, n0 = run % GROUPS, START[run]
                jg, nt = JU * UNITS[g], NT[g]
                js = slice(U0[g] * JU, U0[g] * JU + jg)
                link(dve.tensor_tensor(tcmp[:, 0:nt, :], t_iota[:, 0:nt, :],
                                       ne[:, 2, None, :].to_broadcast([P, nt, E]), ALU.is_ge))
                te = teid[:, n0 + 1:n0 + nt + 1]
                link(dve.tensor_reduce(te, tcmp[:, 0:nt, :], AX.X, ALU.add))
                link(dve.tensor_scalar(te, te, float(E - 1), None, ALU.min))
                dve.scalar_tensor_tensor(eid[:, n0:n0 + nt], teid[:, n0:n0 + nt], float(E), te, ALU.mult, ALU.add)
                dve.wait_ge(s_ed, run + 1)
                link(dve.tensor_scalar(mx[0][:, 0:jg], ed[:, 0, 0:jg], 2.0, 2.0, ALU.mult, ALU.add))
                link(dve.reciprocal(mx[1][:, 0:jg], mx[0][:, 0:jg]))
                link(dve.tensor_scalar(wts[:, 0, js], mx[1][:, 0:jg], 1.0 / WS, None, ALU.mult))
                dve.tensor_tensor(wts[:, 1, js], wts[:, 0, js], ed[:, 0, 0:jg], ALU.mult).then_inc(s_routed, 1)

            def weights():
                dve.wait_ge(s_small, 16 * 3)
                dve.wait_ge(s_wexp, 1)
                dve.tensor_scalar(omix[:], vecs[:, 0:3], -1.0, 1.0, ALU.mult, ALU.add)
                link(dve.tensor_scalar(wdec[:, 0:1], wdec[:, 0:1], -1.0, None, ALU.mult))
                dve.tensor_tensor(wdec[:, 1:2], wdec[:, 0:1], vecs[:, 4:5], ALU.add)
                dve.tensor_scalar(wfull[:], wfull[:], wdec[:, 0:1], None, ALU.add)
                for i in range(3):
                    dve.tensor_scalar(qkv_f[:, i, :], att_raw[:, i, :], vecs[:, i:i + 1], None, ALU.mult)
                    ins = dve.tensor_scalar(qkv_f[:, 3 + i, :], att_raw[:, i, :], omix[:, i:i + 1], None, ALU.mult)
                ins.then_inc(s_qf, 1)
                with dve.Fori(0, E // WRING) as i:
                    for k in range(WRING):
                        e = i * WRING + k
                        dve.wait_ge(s_uphi, e + 1)
                        dve.scalar_tensor_tensor(
                            up_w[:, bass.ds(e, 1), 1::2, :].rearrange("p e a f -> p (e a) f"), stage_w[:, :, k, :], WS,
                            up_w[:, bass.ds(e, 1), 0::2, :].rearrange("p e a f -> p (e a) f"),
                            ALU.mult, ALU.subtract).then_inc(s_uplo, 1)
                dve.wait_ge(s_qf, 1)
                dve.wait_ge(s_qhi, 1)
                dve.scalar_tensor_tensor(qkv_w[:, :, 1, :], qkv_f[:], WS, qkv_w[:, :, 0, :],
                                         ALU.mult, ALU.subtract).then_inc(s_qlo, 1)

            def half(n, k):
                dve.wait_ge(s_sil, n + 1)
                wait(dve, s_y, n - RING + 1)
                dve.tensor_tensor(h[:, k, :, :].rearrange("p c t -> p (c t)"), sil[:, k % 2, :], pb[k % 2][:],
                                  ALU.mult).then_inc(s_h, 1)

            def combine(run, b):
                g, (u, js) = run % GROUPS, units(run, b)
                runs = [p[2] for p in PLAN if p[1] == "gather" and p[3] == b]
                dve.wait_ge(s_gat[b], 16 * TOPK * JU * (runs.index(run) + 1))
                for c in range(TOPK):
                    for j in range(JU):
                        xj = xres[:, js, :][:, j, :]
                        ins = dve.scalar_tensor_tensor(xj, yg[:, b, c, j, :], wts[:, c, u * JU + j:u * JU + j + 1],
                                                       xj, ALU.mult, ALU.add)
                    if c == 0:
                        link(ins)
                ins.then_inc(s_comb, 1)
                dve.wait_ge(s_comb, count(("combine",), ("combine", run, b)))

            def step(name, run, b):
                u, _ = units(run, b)
                k, v, r = kk[:, u % 2, :], vv[:, u % 2, :], er[:, u % 2, :]
                if name == "combine":
                    combine(run, b)
                if name in ("stats", "mstats"):
                    if name == "stats" and run < GROUPS:
                        dve.wait_ge(s_x[run], 16 * (UNITS[0] if run == 0 else 1))
                    statistics(run, b)
                if name in NORMS:
                    normalise(name, run, b)
                if name in ("lo", "lo_m"):
                    parts_lo(name, run, b)
                if name == "pick":
                    pick_expert(run, 0)
                if name == "pick2":
                    pick_expert(run, 1)
                if name == "place":
                    place(run)
                if name == "tiles":
                    tiles_and_weights(run)
                if name == "peak":
                    dve.wait_ge(s_bread, count(B_STEPS, ("pk", run, b)))
                    link(dve.tensor_tensor_scan(pp[:, 1:], wfull[:], k, NEG, ALU.add, ALU.max))
                    link(dve.scalar_tensor_tensor(dd[:], pp[:, 0:S], vecs[:, 4:5], k, ALU.subtract, ALU.subtract))
                if name == "gaps":
                    wait(dve, s_exp, count(("exps2",), ("exps2", run, b)) - 1)
                    dve.tensor_scalar(mn[:, 0, :], dd[:], 0.0, None, ALU.min)
                    dve.tensor_scalar(mxx[:, 0, :], dd[:], 0.0, None, ALU.max)
                    dve.tensor_scalar(mn[:, 1, :], dd[:], wdec[:, 1:2], 0.0, ALU.add, ALU.min)
                    dve.tensor_scalar(mxx[:, 1, :], dd[:], wdec[:, 1:2], 0.0, ALU.add, ALU.max).then_inc(s_min, 1)
                if name == "sum_a":
                    dve.wait_ge(s_exp, count(("exps2",), ("exps2", run, b)))
                    dve.wait_ge(s_aread, count(A_STEPS, ("pv", run, b)))
                    link(dve.tensor_tensor(kv[:], e2[:, 1, :], v, ALU.mult))
                    link(dve.tensor_tensor_scan(aa[:, 1:], e1[:, 1, :], kv[:], 0.0, ALU.mult, ALU.add))
                if name == "sum_b":
                    link(dve.tensor_tensor_scan(bb[:, 1:], e1[:, 1, :], e2[:, 1, :], 0.0, ALU.mult, ALU.add))
                    dve.tensor_tensor(num[:], e1[:, 0, :], aa[:, 0:S], ALU.mult)
                if name == "weigh":
                    dve.tensor_tensor(tm[:], e2[:, 0, :], v, ALU.mult)
                    link(dve.tensor_tensor(den[:], e1[:, 0, :], bb[:, 0:S], ALU.mult))
                if name == "total":
                    dve.tensor_tensor(num[:], num[:], tm[:], ALU.add)
                    dve.tensor_tensor(den[:], den[:], e2[:, 0, :], ALU.add).then_inc(s_sums, 1)
                    dve.wait_ge(s_sums, count(("total",), ("total", run, b)))
                if name == "divide":
                    dve.wait_ge(s_bread, count(B_STEPS, ("pr", run, b)))
                    link(dve.scalar_tensor_tensor(den[:], r, 1.0, den[:], ALU.add, ALU.mult))
                    link(dve.reciprocal(tm[:, 0:S // 4], den[:, 0:S // 4]))
                if name == "divide2":
                    link(dve.reciprocal(tm[:, S // 4:3 * S // 4], den[:, S // 4:3 * S // 4]))
                if name == "att":
                    link(dve.reciprocal(tm[:, 3 * S // 4:], den[:, 3 * S // 4:]))
                    dve.tensor_tensor(att[:], num[:], tm[:], ALU.mult).then_inc(s_att, 1)
                if name == "add":
                    u, js = units(run, b)
                    at = count(A_STEPS, ("out", run, b))
                    dve.wait_ge(s_afull, at)
                    dve.tensor_tensor(xres[:, js, :], xres[:, js, :], bkA[:].rearrange("p (j d) -> p j d", d=D),
                                      ALU.add).then_inc(s_aread, 1)
                    dve.wait_ge(s_aread, at)

            in_order(dve, half, step, before_halves=weights, halves=HALVES)
            last_steps(step)

        @block.tensor
        def _(pe):
            pe.wait_ge(s_const, 7)
            up_bytes = up_w[:].rearrange("p e a f -> p (e a f)").bitcast(U8)
            down_bytes = down_w[:].rearrange("p e c d -> p (e c d)").bitcast(U8)

            def turn_tile(t, slot):
                loads = t // SLOTS + 1 if isinstance(t, int) else (t - slot) // SLOTS + 1
                pe.wait_ge(s_rin[slot], 16 * loads)
                wait(pe, s_rT, t)
                for part in range(2):
                    for hh in range(TH):
                        mm = pe.transpose(pT[:, part, hh * P:(hh + 1) * P],
                                          rin[:, slot, hh, part * D:(part + 1) * D], ident16[:])
                mm.then_inc(s_turn, 1)

            def up_chunk(k, c, e):
                for bank, w in ((pa[k % 2], 0), (pb[k % 2], 2)):
                    for i, (wp, xp) in enumerate(((0, 0), (0, 1), (1, 0))):
                        at = 2 * ((w + wp) * F + (k % 2 * (FC // 2) + c) * P)
                        mm = pe.matmul(bank[:, c * T:(c + 1) * T],
                                       up_bytes[:, bass.ds(e * (2 * 4 * F) + at, 2 * P)].bitcast(F16),
                                       rT[:, k // 2, xp, :], start=(i == 0), stop=(i == 2))
                return mm

            def down(n, k, e):
                pe.wait_ge(s_h, n + 1)
                if k % 2 == 0:
                    wait(pe, s_yrow, tile_of(n, k)[0])
                for c in range(FC // 2):
                    at = 4 * (k % 2 * (FC // 2) + c) * D
                    w = down_bytes[:, bass.ds(e * (4 * FC * D) + at, 4 * D)].bitcast(F32)
                    for hh in range(TH):
                        mm = pe.matmul(py[:, hh, :], h[:, k, c, hh * P:(hh + 1) * P], w,
                                       start=(k % 2 == 0 and c == 0 and hh == 0),
                                       stop=(k % 2 == 1 and c == FC // 2 - 1), skip_group_check=True)
                mm.then_inc(s_y, 1)

            experts = [None] * SLOTS

            def load_expert(t, slot):
                both = pe.value_load(eid[0:1, bass.ds(t, 1)], min_val=0, max_val=E * E - 1)
                experts[slot] = pe.snap(both % E, min_val=0, max_val=E - 1)
                return both

            def half(n, k):
                t, slot = tile_of(n, k)
                looped = not isinstance(n, int)
                if not looped and k % 2 == 0 and t in START:
                    pe.wait_ge(s_routed, START.index(t) + 1)
                if k % 2 == 0 and not (looped and k == 2):
                    both = load_expert(t, slot)
                    if looped or n == HALVES - RING:
                        experts[-1] = pe.snap(both // E, min_val=0, max_val=E - 1)
                if k % 2 == 0:
                    pe.wait_ge(s_rT, t + 1)
                wait(pe, s_h, n - 1)
                up_chunk(k, 0, experts[slot])
                if k % 2 == 0 and not (isinstance(n, int) and n == HALVES - 2):
                    turn_tile(t + 1, (slot + 1) % SLOTS)
                up_chunk(k, 1, experts[slot]).then_inc(s_up, 1)
                if looped and k == 1:
                    nxt = pe.value_load(eid[0:1, bass.ds(t + 1, 1)], min_val=0, max_val=E * E - 1)
                if not (isinstance(n, int) and n < 2):
                    down(n - 2, (k - 2) % RING, experts[slot - 1])
                if looped and k == 1:
                    experts[1] = pe.snap(nxt % E, min_val=0, max_val=E - 1)

            def bank_free(s_read, uses):
                wait(pe, s_read, uses - 1)

            def project(u, i, bank):
                n = 0
                for f, start in ((i, 2), (3 + i, 1)):
                    for wp, xp in ((0, 0), (0, 1), (1, 0)):
                        mm = pe.matmul(bank[:], qkv_w[:, f, wp, :], xT[:, u % 2, xp, start:start + S],
                                       start=(n == 0), stop=(n == 5))
                        n += 1
                return mm

            def step(name, run, b):
                u, js = units(run, b)
                me = (name, run, b)
                if name in A_STEPS:
                    bank_free(s_aread, count(A_STEPS, me))
                if name in B_STEPS:
                    bank_free(s_bread, count(B_STEPS, me))
                if name == "turn":
                    pe.wait_ge(s_xn, count(NORMS, ("norm", run, b)))
                    for j in range(JU):
                        mm = pe.transpose(bkA[:, j * P:(j + 1) * P], xn[:, xn_slot("norm", run, b), j, :], ident[:])
                    mm.then_inc(s_afull, 1)
                if name == "logits":
                    pe.wait_ge(s_small, 16 * 3)
                    pe.wait_ge(s_aread, count(A_STEPS, ("turn", run, b)))
                    for j in range(JU):
                        mm = pe.matmul(bkB[:, j * E:(j + 1) * E], xnT[:, j * P:(j + 1) * P], gate_w[:],
                                       start=True, stop=True)
                    mm.then_inc(s_bfull, 1)
                if name == "count":
                    pe.wait_ge(s_chosen, run + 1)
                    cols = UNITS[run % GROUPS] * JU * E
                    cv = chosen[:].rearrange("p j e -> p (j e)")[:, 0:cols]
                    pe.matmul(bkB[:, 0:cols], ones16[:], cv, start=True, stop=True).then_inc(s_bfull, 1)
                    pe.matmul(bkA[:, 0:cols], upper[:], cv, start=True, stop=True).then_inc(s_afull, 1)
                if name == "turn_m":
                    pe.wait_ge(s_lo, count(("lo", "lo_m"), ("lo_m", run, b)))
                    a16 = bkA[:].bitcast(F16)
                    for part in range(2):
                        for j in range(JU):
                            mm = pe.transpose(a16[:, part * S + j * P:part * S + (j + 1) * P],
                                              parts[:, u * JU + j, part * D:(part + 1) * D], ident16[:])
                    mm.then_inc(s_afull, 1)
                if name == "pk":
                    pe.wait_ge(s_qlo, 1)
                    pe.wait_ge(s_aread, count(A_STEPS, ("turn_m", run, b)))
                    project(u, 0, bkB).then_inc(s_bfull, 1)
                if name == "pv":
                    project(u, 1, bkA).then_inc(s_afull, 1)
                if name == "pr":
                    project(u, 2, bkB).then_inc(s_bfull, 1)
                if name == "out":
                    pe.wait_ge(s_att, count(("att",), ("att", run, b)))
                    for j in range(JU):
                        mm = pe.matmul(bkA[:, j * P:(j + 1) * P], att[:, j * P:(j + 1) * P], att_raw[:, 3, :],
                                       start=True, stop=True)
                    mm.then_inc(s_afull, 1)

            def weights_in():
                turn_tile(0, 0)
                pe.wait_ge(s_uplo, E + WRING)
                pe.wait_ge(s_w2, 16)

            in_order(pe, half, step, before_halves=weights_in, halves=HALVES - RING)
            for n in range(HALVES - RING, HALVES):
                half(n, n % RING)
            for n in range(HALVES - 2, HALVES):
                down(n, n % RING, experts[(TILES - 1) % SLOTS])


def kernel(L0_attn_x, L0_attn_time_mix_k, L0_attn_time_mix_v, L0_attn_time_mix_r, L0_attn_time_decay,
           L0_attn_time_first, L0_attn_Wk, L0_attn_Wv, L0_attn_Wr, L0_attn_Wo, L0_ffn_gate_w, L0_ffn_w1,
           L0_ffn_w3, L0_ffn_w2):
    import numpy as np
    import concourse.bacc as bacc
    from concourse.bass_utils import run_bass_kernel_spmd

    vec = [L0_attn_time_mix_k, L0_attn_time_mix_v, L0_attn_time_mix_r, L0_attn_time_decay, L0_attn_time_first]
    arrays = {
        "x": np.ascontiguousarray(L0_attn_x),
        "channel_vecs": np.ascontiguousarray(np.stack([np.asarray(v).reshape(D) for v in vec], axis=1)),
        "att_w": np.ascontiguousarray(np.stack(
            [np.asarray(w).T for w in (L0_attn_Wk, L0_attn_Wv, L0_attn_Wr, L0_attn_Wo)], axis=1)),
        "gate": np.ascontiguousarray(L0_ffn_gate_w),
        "w1": np.ascontiguousarray(L0_ffn_w1),
        "w3": np.ascontiguousarray(L0_ffn_w3),
        "w2": np.ascontiguousarray(L0_ffn_w2),
    }
    nc = bacc.Bacc("TRN2", target_bir_lowering=False, num_devices=1)
    args = [nc.dram_tensor(f"in_{n}", a.shape, mybir.dt.from_np(a.dtype), kind="ExternalInput").ap()
            for n, a in arrays.items()]
    out = nc.dram_tensor("out_0", (B, S, D), F32, kind="ExternalOutput").ap()
    macaron_kernel(nc, *args, out)
    r = run_bass_kernel_spmd(nc, [{f"in_{n}": a for n, a in arrays.items()}], core_ids=[0])
    return r.results[0]["out_0"]
```

```python
from collections import Counter, namedtuple
from contextlib import ExitStack

import concourse.bass as bass
from concourse import mybir

ALU = mybir.AluOpType
ACT = mybir.ActivationFunctionType
AX = mybir.AxisListType
F32 = mybir.dt.float32
F16 = mybir.dt.float16
BF16 = mybir.dt.bfloat16
I32 = mybir.dt.int32
U8 = mybir.dt.uint8

P = 128
B, S, D = 8, 512, 128
E, F, TOPK = 8, 512, 2
FC = F // P
JU = S // P
UNITS = (3, 3, 2)
GROUPS = len(UNITS)
U0 = tuple(sum(UNITS[:g]) for g in range(GROUPS))
UG = max(UNITS)
JG = UG * JU
T = 256
TH = T // P
NT = tuple((u * S * TOPK + E * (T - 1)) // T for u in UNITS)
RUNS = 2 * GROUPS
START = tuple(sum(NT[q % GROUPS] for q in range(r)) for r in range(RUNS + 1))
TILES = START[RUNS]
HALVES = 2 * TILES
EPS = 1e-5
WS = 64.0
MAGIC = 0x5F3759DF
NEG = -1e30
BIG = 3e38

WRING = 4
XSLOTS = 3
SLOTS = 2
RING = 2 * SLOTS
LOOPED = 168

NORM = [("stats", 0), ("rsqrt", 1), ("norm", 2), ("hi", 3), ("lo", 4), ("turn", 4), ("xnT", 5), ("logits", 6),
        ("keep", 7)]
MIX = [("combine", 0), ("mstats", 1), ("mrsqrt", 2), ("mnorm", 3), ("hi_m", 4), ("lo_m", 5), ("turn_m", 6),
       ("xT", 7), ("pk", 8), ("k", 9), ("pv", 9), ("v", 10), ("pr", 10), ("peak", 10), ("gaps", 11), ("r", 11),
       ("exps", 12), ("exps2", 12), ("sum_a", 14), ("sum_b", 15), ("weigh", 16), ("total", 17), ("divide", 18),
       ("divide2", 19), ("att", 20), ("out", 21), ("add", 22)]
CHOOSE = [("pick", 0), ("pick2", 1), ("count", 2), ("place", 3), ("place2", 4), ("scatter", 5), ("tiles", 5),
          ("weights", 6)]
MIX_DONE = [step for step, _ in MIX].index("att") + 1

HOLDS = [("turn", "A", "xnT"), ("turn_m", "A", "xT"), ("pv", "A", "v"), ("out", "A", "add"), ("count", "A", "place2"),
         ("logits", "B", "keep"), ("pk", "B", "k"), ("pr", "B", "r"), ("count", "B", "place"),
         ("norm", "xn", "lo"), ("mnorm", "xn", "lo_m"), ("xnT", "xnT", "keep"), ("pick", "routing", "weights"),
         ("peak", "gaps", "exps2"), ("exps", "exps", "total"), ("sum_a", "sums", "att")]

COST = {"dve": {"combine": 1.5, "stats": 1.2, "mstats": 1.2, "rsqrt": 1.5, "mrsqrt": 1.5, "norm": 1.3, "mnorm": 1.3,
                "lo": 0.6, "lo_m": 0.6, "peak": 1.2, "gaps": 1.4, "sum_a": 1.2, "sum_b": 1.2, "weigh": 1.2,
                "total": 1.2, "divide": 1.5, "divide2": 1.7, "att": 1.5, "add": 0.6, "pick": 1.3, "pick2": 1.3,
                "place": 2.2, "place2": 1.2, "tiles": 0.8, "weights": 0.9},
        "act": {"hi": 0.5, "hi_m": 0.5, "xnT": 0.5, "keep": 0.2, "xT": 1.0, "k": 0.5, "v": 0.5, "r": 0.5,
                "exps": 1.7, "exps2": 1.7, "count": 2.6}}
ROOM = {"dve": 2.9, "act": 4}


Chain = namedtuple("Chain", "steps run unit start follows done")


def make_plan():
    chains = []

    def chain(steps, run, b, first, follows=()):
        chains.append(Chain(steps, run, b, first, list(follows), []))
        return chains[-1]

    def route(run, normed):
        chain(CHOOSE, run, 0, 0, normed)

    for run in range(1, GROUPS):
        route(run, [chain(NORM, run, b, 0) for b in range(UNITS[run])])
    for g in range(GROUPS):
        stored = 2 * START[g + 1] + 2
        mixed = [chain(MIX, g, b, stored + 3 + 4 * b) for b in range(UNITS[g])]
        route(GROUPS + g, [chain(NORM, GROUPS + g, b, 0, [mixed[b]]) for b in range(UNITS[g])])
    for g in range(GROUPS - 1):
        stored = 2 * START[GROUPS + g + 1] + 2
        for b in range(UNITS[g]):
            chain([("combine", 0), ("write", 3)], GROUPS + g, b, stored + 3 + 4 * b)

    first = range(UNITS[0])
    plan = [(-1, "stats", 0, b) for b in first] + [(-1, "rsqrt", 0, 0)]
    plan += [(-1, "norm", 0, b) for b in first]
    plan += [(-1, step, 0, b) for b in first for step in ("turn", "xnT", "logits", "keep")]
    plan += [(-1, "hi", 0, b) for b in first] + [(-1, "pick", 0, 0), (-1, "pick2", 0, 0), (-1, "count", 0, 0)]
    plan += [(-1, "lo", 0, b) for b in first]
    plan += [(-1, step, 0, 0) for step, _ in CHOOSE[3:]]

    held = {}
    for half in range(HALVES):
        load, wanted = Counter(), set()
        for g in range(RUNS - 1):
            if half == 2 * START[g + 1] + 2:
                plan += [(half, "gather", g, b) for b in range(UNITS[g % GROUPS])]
        for k, (steps, run, b, start, follows, done) in enumerate(chains):
            lane = [c for c in chains[:k] if c.steps is steps]
            while len(done) < len(steps):
                step, at = steps[len(done)]
                due = done[-1] + at - steps[len(done) - 1][1] if done else start
                takes = [what for name, what, _ in HOLDS if name == step]
                frees = [what for _, what, name in HOLDS if name == step]
                if (half < due or any(len(c.done) <= len(done) for c in lane[-1:])
                        or any(len(c.done) < len(c.steps) or c.done[-1] >= half for c in follows)):
                    break
                if wanted & set(takes):
                    break
                if any(held.get(what) is not None for what in takes if what not in frees):
                    wanted.update(takes)
                    break
                if (step == "xT" and any(c.done and len(c.done) < MIX_DONE for c in lane[:-1])
                        or step == "keep" and any(len(c.done) < 2 or c.done[1] >= half for c in chains
                                                  if c.steps is CHOOSE and c.run < run)
                        or any(load[eng] and load[eng] + COST[eng].get(step, 0) > ROOM[eng] for eng in COST
                               if step in COST[eng])):
                    break
                for what in frees:
                    held[what] = None
                for what in takes:
                    held[what] = k
                for eng in COST:
                    load[eng] += COST[eng].get(step, 0)
                done.append(half)
                plan.append((half, step, run, b))
    assert all(len(c.done) == len(c.steps) for c in chains)
    last = [(HALVES, step, RUNS - 1, b) for step in ("gather", "combine", "write") for b in range(UNITS[-1])]
    return plan + last


PLAN = make_plan()


def count(steps, upto):
    order = [p[1:] for p in PLAN if p[1] in steps]
    return order.index(upto) + 1


def wait(eng, sem, value):
    if not isinstance(value, int) or value > 0:
        eng.wait_ge(sem, value)


def in_order(eng, half, step, halves, before_halves=None):
    for _, name, run, b in (p for p in PLAN if p[0] < 0):
        step(name, run, b)
    if before_halves:
        before_halves()
    for n in range(LOOPED):
        half(n, n % RING)
        for _, name, run, b in (p for p in PLAN if p[0] == n):
            step(name, run, b)
    at = LOOPED
    stops = sorted({-(-p[0] // RING) * RING for p in PLAN if LOOPED <= p[0] < HALVES} | {halves})
    for stop in stops:
        if stop > at:
            with eng.Fori(at // RING, stop // RING) as i:
                for k in range(RING):
                    half(i * RING + k, k)
            at = stop
        for _, name, run, b in (p for p in PLAN if LOOPED <= p[0] < HALVES and -(-p[0] // RING) * RING == stop):
            step(name, run, b)


def last_steps(step):
    for _, name, run, b in (p for p in PLAN if p[0] == HALVES):
        step(name, run, b)


def macaron_kernel(nc, x, channel_vecs, att_w, gate, w1, w3, w2, out):
    with ExitStack() as ctx:
        def sb(name, shape, dt=F32):
            return ctx.enter_context(nc.sbuf_tensor(name, shape, dt))

        def ps(name, shape, dt=F32):
            return ctx.enter_context(nc.psum_tensor(name, shape, dt))

        def sem(name):
            return ctx.enter_context(nc.semaphore(name))

        rows_in = [nc.dram_tensor(f"rows_in{g}", (NT[g] * T, 2 * D), F16, kind="Internal").ap() for g in range(GROUPS)]
        rows_out = [nc.dram_tensor(f"rows_out{g}", (NT[g] * T, D), F32, kind="Internal").ap() for g in range(GROUPS)]

        xres = sb("xres", [P, B * JU, D])
        up_w = sb("up_w", [P, E, 4, F], F16)
        down_w = sb("down_w", [P, E, FC, D])
        stage_w = sb("stage_w", [P, 2, WRING, F])
        gate_w = sb("gate_w", [P, E])
        att_raw = sb("att_raw", [P, 4, D])
        qkv_f = sb("qkv_f", [P, 6, D])
        qkv_w = sb("qkv_w", [P, 6, 2, D], F16)
        vecs = sb("vecs", [P, 5])
        omix = sb("omix", [P, 3])
        wdec = sb("wdec", [P, 2])
        wfull = sb("wfull", [P, S])
        ident = sb("ident", [P, P])
        ident16 = sb("ident16", [P, P], F16)
        upper = sb("upper", [P, P], BF16)
        ones16 = sb("ones16", [P, P], BF16)
        zrow = sb("zrow", [P, 2 * D], F16)
        e_desc = sb("e_desc", [P, JG, E])
        t_iota = sb("t_iota", [P, max(NT), E])
        stats = sb("stats", [P, JU, 6])
        mv = sb("mv", [P, B, JU, 2])
        var = sb("var", [P, B, JU])
        bits = sb("bits", [P, B, JU], I32)
        rstd = sb("rstd", [P, B, JU])
        nwt = sb("nwt", [P, B, JU])
        xn = sb("xn", [P, XSLOTS, JU, D])
        parts = sb("parts", [P, B * JU, 2 * D], F16)
        xnT = sb("xnT", [P, S])
        logit = sb("logit", [P, JG, E])
        rt = [sb(f"rt{i}", [P, JG, E]) for i in range(3)]
        pick = [sb(f"pick{i}", [P, JG, E]) for i in range(2)]
        mx = [sb(f"mx{i}", [P, JG]) for i in range(2)]
        kx = sb("kx", [P, JG])
        chosen = sb("chosen", [P, JG, E], BF16)
        cnt = sb("cnt", [P, E * JG])
        run_s = sb("run_s", [P, E * JG])
        one_s = sb("one_s", [P, E * JG])
        ne = sb("ne", [P, 6, E])
        nei = sb("nei", [P, E], I32)
        tcmp = sb("tcmp", [P, max(NT), E])
        teid = sb("teid", [P, TILES + 1])
        slotf = sb("slotf", [P, 2, JG])
        slot = sb("slot", [P, 2, B * JU], I32)
        wts = sb("wts", [P, 2, B * JU])
        ed = sb("ed", [P, 2, JG])
        eid = sb("eid", [P, TILES], I32)
        rin = sb("rin", [P, SLOTS, TH, 2 * D], F16)
        rT = sb("rT", [P, SLOTS, 2, T], F16)
        sil = sb("sil", [P, 2, FC // 2 * T])
        h = sb("h", [P, RING, FC // 2, T])
        yrow = sb("yrow", [P, SLOTS, TH, D])
        yg = sb("yg", [P, UG, TOPK, JU, D])
        xT = sb("xT", [P, 2, 2, S + 2], F16)
        kk = sb("kk", [P, 2, S])
        vv = sb("vv", [P, 2, S])
        tr = sb("tr", [P, 2, S])
        pp = sb("pp", [P, S + 1])
        dd = sb("dd", [P, S])
        mn = sb("mn", [P, 2, S])
        mxx = sb("mxx", [P, 2, S])
        e1 = sb("e1", [P, 2, S])
        e2 = sb("e2", [P, 2, S])
        kv = sb("kv", [P, S])
        aa = sb("aa", [P, S + 1])
        bb = sb("bb", [P, S + 1])
        num = sb("num", [P, S])
        den = sb("den", [P, S])
        tm = sb("tm", [P, S])
        att = sb("att", [P, S])

        pa = [ps(f"pa{q}", [P, FC // 2 * T]) for q in range(2)]
        pb = [ps(f"pb{q}", [P, FC // 2 * T]) for q in range(2)]
        pT = ps("pT", [P, 2, T], F16)
        py = ps("py", [P, TH, D])
        bkA = ps("bkA", [P, S])
        bkB = ps("bkB", [P, S])

        s_x = [sem(f"x_in{g}") for g in range(GROUPS)]
        s_small = sem("small_in")
        s_stage = [sem(f"stage_in{i}") for i in range(WRING)]
        s_w2 = sem("w2_in")
        s_zrow = sem("zrow_made")
        s_fill = [sem(f"rows_zeroed{g}") for g in range(GROUPS)]
        s_const = sem("const_made")
        s_uphi = sem("up_hi_made")
        s_uplo = sem("up_lo_made")
        s_qf = sem("qkv_folded")
        s_qhi = sem("qkv_hi_made")
        s_qlo = sem("qkv_lo_made")
        s_wexp = sem("decay_exp_made")
        s_chain = sem("dve_chain")
        s_xn = sem("xn_made")
        s_hi = sem("parts_hi_made")
        s_lo = sem("parts_lo_made")
        s_afull = sem("bankA_full")
        s_aread = sem("bankA_read")
        s_bfull = sem("bankB_full")
        s_bread = sem("bankB_read")
        s_chosen = sem("chosen_made")
        s_ed = sem("gap_exp_made")
        s_slots = sem("slots_made")
        s_eid = sem("tile_experts_made")
        s_scat = [sem(f"scattered{g}") for g in range(GROUPS)]
        s_rin = [sem(f"tile_in{i}") for i in range(SLOTS)]
        s_turn = sem("tile_turned")
        s_rT = sem("tile_copied")
        s_up = sem("up_done")
        s_sil = sem("silu_done")
        s_h = sem("h_made")
        s_y = sem("down_done")
        s_yrow = sem("y_copied")
        s_yst = [sem(f"y_stored{i}") for i in range(SLOTS)]
        s_gat = [sem(f"gathered{b}") for b in range(UG)]
        s_comb = sem("combined")
        s_min = sem("minmax_made")
        s_exp = sem("exps_made")
        s_sums = sem("sums_made")
        s_att = sem("att_made")
        s_out = sem("out_stored")

        block = ctx.enter_context(nc.Block())

        A_STEPS = ("turn", "turn_m", "pv", "out", "count")
        B_STEPS = ("logits", "pk", "pr", "count")
        NORMS = ("norm", "mnorm")
        SPLITS = {"norm": "hi", "mnorm": "hi_m"}

        def units(run, b):
            u = U0[run % GROUPS] + b
            return u, slice(u * JU, (u + 1) * JU)

        def tile_of(n, k):
            return (n - k) // 2 + k // 2, k // 2

        def xn_slot(name, run, b):
            return (count(NORMS, (name, run, b)) - 1) % XSLOTS

        @block.sync
        def _(sp):
            xv = x.rearrange("b (j p) d -> p (b j) d", p=P)
            ov = out.rearrange("b (j p) d -> p (b j) d", p=P)
            for u in range(UNITS[0]):
                sp.dma_start(xres[:, u * JU:(u + 1) * JU, :], xv[:, u * JU:(u + 1) * JU, :]).then_inc(s_x[0], 16)
            sp.dma_start(gate_w[:], gate).then_inc(s_small, 16)
            sp.dma_start(vecs[:], channel_vecs).then_inc(s_small, 16)
            sp.dma_start(att_raw[:], att_w).then_inc(s_small, 16)

            def fill(g):
                sp.dma_start(rows_in[g].rearrange("(p r) c -> p r c", p=P),
                             zrow[:, None, :].to_broadcast([P, NT[g] * TH, 2 * D])).then_inc(s_fill[g], 16)

            sp.wait_ge(s_zrow, 1)
            fill(0)

            def stage(k, e):
                for n, a in enumerate((w1, w3)):
                    sp.dma_start(stage_w[:, n, k, :], a[bass.ds(e, 1), :, :].rearrange("e d f -> d (e f)")
                                 ).then_inc(s_stage[k], 16)

            for k in range(WRING):
                stage(k, k)
            sp.dma_start(down_w[:], w2.rearrange("e (c p) d -> p e c d", p=P)).then_inc(s_w2, 16)
            for g in range(1, GROUPS):
                js = slice(U0[g] * JU, (U0[g] + UNITS[g]) * JU)
                sp.dma_start(xres[:, js, :], xv[:, js, :]).then_inc(s_x[g], 16)
                fill(g)
            for e in range(WRING, E):
                sp.wait_ge(s_uplo, e - WRING + 1)
                stage(e % WRING, e)

            def rows(tensors, t):
                run = max(r for r in range(RUNS) if START[r] <= t)
                i = t - START[run]
                return tensors[run % GROUPS][i * T:(i + 1) * T, :].rearrange("(h p) c -> p h c", p=P)

            def load(t):
                if t in START:
                    run = START.index(t)
                    sp.wait_ge(s_scat[run % GROUPS], 16 * TOPK * JU * UNITS[run % GROUPS] * (run // GROUPS + 1))
                wait(sp, s_turn, t - SLOTS + 1)
                sp.dma_start(rin[:, t % SLOTS, :, :], rows(rows_in, t)).then_inc(s_rin[t % SLOTS], 16)

            def store(t):
                sp.wait_ge(s_yrow, t + 1)
                sp.dma_start(rows(rows_out, t), yrow[:, t % SLOTS, :, :]).then_inc(s_yst[t % SLOTS], 16)

            def step(name, run, b):
                if name == "write":
                    u, js = units(run, b)
                    sp.wait_ge(s_comb, count(("combine",), ("combine", run, b)))
                    sp.dma_start(ov[:, js, :], xres[:, js, :]).then_inc(s_out, 16)

            for t in range(SLOTS):
                load(t)
            for t in range(TILES + 1):
                if t + SLOTS < TILES:
                    load(t + SLOTS)
                if t >= 1:
                    store(t - 1)
                for _, name, run, b in (p for p in PLAN if p[0] in (2 * t, 2 * t + 1)):
                    step(name, run, b)
            sp.wait_ge(s_out, 16 * B)

        @block.gpsimd
        def _(pool):
            pool.memset(ident[:], 0.0).then_inc(s_const, 1)
            pool.memset(upper[:], 0.0).then_inc(s_const, 1)
            pool.wait_ge(s_const, 2)
            pool.affine_select(out=ident[:], in_=ident[:], compare_op=ALU.not_equal, fill=1.0, base=0,
                               pattern=[[-1, P]], channel_multiplier=1).then_inc(s_const, 1)
            pool.affine_select(out=upper[:], in_=upper[:], compare_op=ALU.is_ge, fill=1.0, base=0,
                               pattern=[[-1, P]], channel_multiplier=1).then_inc(s_const, 1)
            pool.wait_ge(s_const, 4)
            pool.tensor_copy(ident16[:], ident[:]).then_inc(s_const, 1)
            pool.iota(e_desc[:], [[0, JG], [-1, E]], E, 0, allow_small_or_imprecise_dtypes=True).then_inc(s_const, 1)
            pool.iota(t_iota[:], [[1, max(NT)], [0, E]], 0, 0, allow_small_or_imprecise_dtypes=True).then_inc(s_const, 1)

            for _, name, run, b in PLAN:
                g = run % GROUPS
                if name == "scatter":
                    pool.wait_ge(s_slots, run + 1)
                    pool.wait_ge(s_lo, max(count(("lo", "lo_m"), ("lo", run, i)) for i in range(UNITS[g])))
                    if run < GROUPS:
                        pool.wait_ge(s_fill[g], 16)
                    for j in range(U0[g] * JU, (U0[g] + UNITS[g]) * JU):
                        for c in range(TOPK):
                            pool.indirect_dma_start(
                                rows_in[g][:], bass.IndirectOffsetOnAxis(ap=slot[:, c, j:j + 1], axis=0),
                                parts[:, j, :], None).then_inc(s_scat[g], 16)
                if name == "gather":
                    _, js = units(run, b)
                    if b == 0:
                        for k in range(SLOTS):
                            pool.wait_ge(s_yst[k], 16 * len(range(k, START[run + 1], SLOTS)))
                    before = [p[1:] for p in PLAN if p[1] == "gather" and p[3] == b]
                    if before.index((name, run, b)):
                        _, last_run, _ = before[before.index((name, run, b)) - 1]
                        pool.wait_ge(s_comb, count(("combine",), ("combine", last_run, b)))
                    for j in range(JU):
                        for c in range(TOPK):
                            pool.indirect_dma_start(
                                yg[:, b, c, j, :], None, rows_out[g][:],
                                bass.IndirectOffsetOnAxis(ap=slot[:, c, js.start + j:js.start + j + 1], axis=0)
                            ).then_inc(s_gat[b], 16)

        @block.scalar
        def _(act):
            act.wait_ge(s_small, 16 * 3)
            act.activation(wdec[:, 0:1], vecs[:, 3:4], ACT.Exp).then_inc(s_wexp, 1)

            def split_weights():
                with act.Fori(0, E // WRING) as i:
                    for k in range(WRING):
                        act.wait_ge(s_stage[k], 32 * i + 32)
                        act.activation(up_w[:, bass.ds(i * WRING + k, 1), 0::2, :].rearrange("p e a f -> p (e a) f"),
                                       stage_w[:, :, k, :], ACT.Copy, scale=WS).then_inc(s_uphi, 1)
                act.wait_ge(s_qf, 1)
                act.activation(qkv_w[:, :, 0, :], qkv_f[:], ACT.Copy, scale=WS).then_inc(s_qhi, 1)

            def copy_T(t, slot, halves_done=0):
                act.wait_ge(s_turn, t + 1)
                wait(act, s_up, halves_done)
                act.activation(rT[:, slot, :, :], pT[:], ACT.Copy).then_inc(s_rT, 1)

            def copy_y(t, slot, rounds):
                act.wait_ge(s_y, 2 * t + 2)
                wait(act, s_yst[slot], 16 * rounds)
                act.activation(yrow[:, slot, :, :], py[:], ACT.Copy).then_inc(s_yrow, 1)

            def half(n, k):
                t, slot = tile_of(n, k)
                if k % 2 == 0 and not (isinstance(n, int) and n == HALVES - 2):
                    copy_T(t + 1, (slot + 1) % SLOTS, n)
                act.wait_ge(s_up, n + 1)
                act.activation(sil[:, k % 2, :], pa[k % 2][:], ACT.Silu, scale=1.0 / WS).then_inc(s_sil, 1)
                if k % 2 and not (isinstance(n, int) and n == 1):
                    copy_y(t - 1, (slot - 1) % SLOTS, (n - k - (RING if k == 1 else 0)) // RING)

            def step(name, run, b):
                u, js = units(run, b)
                me = (name, run, b)
                if name in ("hi", "hi_m"):
                    src = ("norm" if name == "hi" else "mnorm", run, b)
                    act.wait_ge(s_xn, count(NORMS, src))
                    act.activation(parts[:, js, 0:D], xn[:, xn_slot(*src), :, :], ACT.Copy).then_inc(s_hi, 1)
                if name == "xnT":
                    act.wait_ge(s_afull, count(A_STEPS, ("turn", run, b)))
                    wait(act, s_bfull, count(("xnT",), me) and last_logits(run, b))
                    act.activation(xnT[:], bkA[:], ACT.Copy).then_inc(s_aread, 1)
                if name == "keep":
                    act.wait_ge(s_bfull, count(B_STEPS, ("logits", run, b)))
                    wait(act, s_chosen, run)
                    act.activation(logit[:, b * JU:(b + 1) * JU, :],
                                   bkB[:, 0:JU * E].rearrange("p (j e) -> p j e", e=E), ACT.Copy).then_inc(s_bread, 1)
                if name == "count":
                    act.wait_ge(s_chosen, run + 1)
                    jg = JU * UNITS[run % GROUPS]
                    act.activation(ed[:, 0, 0:jg], ed[:, 1, 0:jg], ACT.Exp).then_inc(s_ed, 1)
                if name == "xT":
                    act.wait_ge(s_afull, count(A_STEPS, ("turn_m", run, b)))
                    act.activation(xT[:, u % 2, :, 2:S + 2], bkA[:].bitcast(F16).rearrange("p (h s) -> p h s", h=2),
                                   ACT.Copy).then_inc(s_aread, 1)
                if name == "k":
                    act.wait_ge(s_bfull, count(B_STEPS, ("pk", run, b)))
                    wait(act, s_att, count(("att",), ("att", run, b)) - 2)
                    act.activation(kk[:, u % 2, :], bkB[:], ACT.Copy, scale=1.0 / WS).then_inc(s_bread, 1)
                if name == "v":
                    act.wait_ge(s_afull, count(A_STEPS, ("pv", run, b)))
                    act.activation(vv[:, u % 2, :], bkA[:], ACT.Copy, scale=0.5 / WS).then_inc(s_aread, 1)
                if name == "r":
                    act.wait_ge(s_bfull, count(B_STEPS, ("pr", run, b)))
                    act.activation(tr[:, u % 2, :], bkB[:], ACT.Tanh, scale=0.5 / WS).then_inc(s_bread, 1)
                if name == "exps":
                    act.wait_ge(s_min, count(("gaps",), ("gaps", run, b)))
                    wait(act, s_sums, count(("total",), ("total", run, b)) - 1)
                    act.activation(e1[:], mn[:], ACT.Exp)
                if name == "exps2":
                    act.activation(e2[:], mxx[:], ACT.Exp, scale=-1.0).then_inc(s_exp, 1)

            def last_logits(run, b):
                i = count(("logits",), ("logits", run, b))
                order = [p[1:] for p in PLAN if p[1] == "logits"]
                return count(B_STEPS, order[i - 2]) if i >= 2 else 0

            in_order(act, half, step, before_halves=lambda: (split_weights(), copy_T(0, 0)), halves=HALVES - RING)
            for n in range(HALVES - RING, HALVES):
                half(n, n % RING)
            copy_y(TILES - 1, (TILES - 1) % SLOTS, (TILES - 1) // SLOTS)

        @block.vector
        def _(dve):
            chained = [0]

            def link(ins):
                chained[0] += 1
                ins.then_inc(s_chain, 1)
                dve.wait_ge(s_chain, chained[0])

            dve.memset(zrow[:], 0.0).then_inc(s_zrow, 1)
            dve.memset(ones16[:], 1.0)
            dve.memset(one_s[:], 1.0)
            dve.memset(pp[:, 0:1], NEG)
            dve.memset(aa[:, 0:1], 0.0)
            dve.memset(bb[:, 0:1], 0.0)
            dve.memset(wfull[:], 0.0)
            dve.memset(teid[:], 0.0)
            link(dve.memset(xT[:, :, :, 0:2], 0.0))

            def statistics(run, b):
                u, js = units(run, b)
                for j in range(JU):
                    ins = dve.bn_stats(stats[:, j, :], xres[:, js, :][:, j, :])
                link(ins)
                for j in range(JU):
                    ins = dve.bn_aggr(mv[:, u, j, :], stats[:, j, :])
                link(ins)

            def rsqrt(bs):
                v, r, w = var[:, bs, :], rstd[:, bs, :], nwt[:, bs, :]
                link(dve.tensor_scalar(v, mv[:, bs, :, 1], EPS, None, ALU.add))
                link(dve.tensor_scalar(bits[:, bs, :], v.bitcast(I32), 1, None, ALU.logical_shift_right))
                link(dve.tensor_scalar(r.bitcast(I32), bits[:, bs, :], -1.0, float(MAGIC), ALU.mult, ALU.add))
                for _ in range(3):
                    link(dve.tensor_tensor(w, r, r, ALU.mult))
                    link(dve.scalar_tensor_tensor(w, w, -0.5, v, ALU.mult, ALU.mult))
                    link(dve.scalar_tensor_tensor(r, w, 1.5, r, ALU.add, ALU.mult))

            def normalise(name, run, b):
                u, js = units(run, b)
                i, at = count(NORMS, (name, run, b)), xn_slot(name, run, b)
                if i > XSLOTS:
                    order = [p[1:] for p in PLAN if p[1] in NORMS]
                    old, orun, ob = order[i - XSLOTS - 1]
                    dve.wait_ge(s_hi, count(("hi", "hi_m"), (SPLITS[old], orun, ob)))
                    if old == "norm":
                        dve.wait_ge(s_afull, count(A_STEPS, ("turn", orun, ob)))
                for j in range(JU):
                    ins = dve.tensor_scalar(xn[:, at, j, :], xres[:, js, :][:, j, :], mv[:, u, j, 0:1],
                                            rstd[:, u, j:j + 1],
                                            ALU.subtract, ALU.mult)
                ins.then_inc(s_xn, 1)

            def parts_lo(name, run, b):
                u, js = units(run, b)
                src = ("norm" if name == "lo" else "mnorm", run, b)
                dve.wait_ge(s_xn, count(NORMS, src))
                dve.wait_ge(s_hi, count(("hi", "hi_m"), (SPLITS[src[0]], run, b)))
                dve.tensor_tensor(parts[:, js, D:2 * D], xn[:, xn_slot(*src), :, :], parts[:, js, 0:D],
                                  ALU.subtract).then_inc(s_lo, 1)

            def pick_expert(run, c):
                g = run % GROUPS
                jg = JU * UNITS[g]
                lg, masked, first, picked = logit[:, 0:jg, :], rt[0][:, 0:jg, :], rt[1][:, 0:jg, :], pick[c][:, 0:jg, :]

                def per_token(v):
                    return v[:, 0:jg, None].to_broadcast([P, jg, E])

                if c == 0:
                    dve.wait_ge(s_const, 7)
                    dve.wait_ge(s_bread, max(count(B_STEPS, ("logits", run, b)) for b in range(UNITS[g])))
                src = masked if c else lg
                link(dve.tensor_reduce(mx[c][:, 0:jg], src, AX.X, ALU.max))
                link(dve.tensor_tensor(first, src, per_token(mx[c]), ALU.is_equal))
                link(dve.tensor_tensor(first, first, e_desc[:, 0:jg, :], ALU.mult))
                link(dve.tensor_reduce(kx[:, 0:jg], first, AX.X, ALU.max))
                link(dve.tensor_tensor(picked, e_desc[:, 0:jg, :], per_token(kx), ALU.is_equal))
                if c == 0:
                    link(dve.scalar_tensor_tensor(masked, picked, -BIG, lg, ALU.mult, ALU.add))
                else:
                    wait(dve, s_ed, run)
                    dve.tensor_tensor(ed[:, 1, 0:jg], mx[1][:, 0:jg], mx[0][:, 0:jg], ALU.subtract)
                    dve.tensor_tensor(chosen[:, 0:jg, :], pick[0][:, 0:jg, :], pick[1][:, 0:jg, :],
                                      ALU.add).then_inc(s_chosen, 1)

            def place(run):
                g = run % GROUPS
                jg = JU * UNITS[g]
                cnt_f, run_f = cnt[:, 0:E * jg], run_s[:, 0:E * jg]
                cnt_e, run_e = (v.rearrange("p (e j) -> p e j", e=E) for v in (cnt_f, run_f))
                dve.wait_ge(s_bfull, count(B_STEPS, ("count", run, 0)))
                dve.tensor_copy(cnt_e, bkB[:, 0:jg * E].rearrange("p (j e) -> p e j", e=E)).then_inc(s_bread, 1)
                dve.wait_ge(s_bread, count(B_STEPS, ("count", run, 0)))
                link(dve.tensor_tensor_scan(run_f, one_s[:, 0:E * jg], cnt_f, 0.0, ALU.mult, ALU.add))
                link(dve.tensor_reduce(ne[:, 0, :], cnt_e, AX.X, ALU.add))
                link(dve.tensor_scalar(nei[:], ne[:, 0, :], float(T - 1), None, ALU.add))
                link(dve.tensor_scalar(nei[:], nei[:], T.bit_length() - 1, None, ALU.logical_shift_right))
                link(dve.tensor_copy(ne[:, 1, :], nei[:]))
                link(dve.tensor_tensor_scan(ne[:, 2, :], one_s[:, 0:E], ne[:, 1, :], 0.0, ALU.mult, ALU.add))
                link(dve.tensor_tensor(ne[:, 3, :], ne[:, 2, :], ne[:, 1, :], ALU.subtract))
                link(dve.tensor_tensor(ne[:, 4, :], run_e[:, :, jg - 1], ne[:, 0, :], ALU.subtract))
                link(dve.scalar_tensor_tensor(ne[:, 5, :], ne[:, 3, :], float(T), ne[:, 4, :], ALU.mult, ALU.subtract))
                link(dve.tensor_tensor(run_f, run_f, cnt_f, ALU.subtract))
                link(dve.tensor_tensor(run_e, run_e, ne[:, 5, :, None].to_broadcast([P, E, jg]), ALU.add))

            def place2(run):
                g = run % GROUPS
                jg = JU * UNITS[g]
                js = slice(U0[g] * JU, U0[g] * JU + jg)
                run_e = run_s[:, 0:E * jg].rearrange("p (e j) -> p e j", e=E)
                dve.wait_ge(s_afull, count(A_STEPS, ("count", run, 0)))
                dve.tensor_tensor(rt[0][:, 0:jg, :], bkA[:, 0:jg * E].rearrange("p (j e) -> p j e", e=E),
                                  run_e.rearrange("p e j -> p j e"), ALU.add).then_inc(s_aread, 1)
                dve.wait_ge(s_aread, count(A_STEPS, ("count", run, 0)))
                for c in range(TOPK):
                    link(dve.tensor_tensor(rt[1 + c][:, 0:jg, :], rt[0][:, 0:jg, :], pick[c][:, 0:jg, :], ALU.mult))
                for c in range(TOPK):
                    link(dve.tensor_reduce(slotf[:, c, 0:jg], rt[1 + c][:, 0:jg, :], AX.X, ALU.add))
                dve.tensor_copy(slot[:, :, js], slotf[:, :, 0:jg]).then_inc(s_slots, 1)

            def tiles(run):
                g, n0 = run % GROUPS, START[run]
                nt = NT[g]
                link(dve.tensor_tensor(tcmp[:, 0:nt, :], t_iota[:, 0:nt, :],
                                       ne[:, 2, None, :].to_broadcast([P, nt, E]), ALU.is_ge))
                te = teid[:, n0 + 1:n0 + nt + 1]
                link(dve.tensor_reduce(te, tcmp[:, 0:nt, :], AX.X, ALU.add))
                link(dve.tensor_scalar(te, te, float(E - 1), None, ALU.min))
                dve.scalar_tensor_tensor(eid[:, n0:n0 + nt], teid[:, n0:n0 + nt], float(E), te, ALU.mult,
                                         ALU.add).then_inc(s_eid, 1)

            def expert_weights(run):
                g = run % GROUPS
                jg = JU * UNITS[g]
                js = slice(U0[g] * JU, U0[g] * JU + jg)
                dve.wait_ge(s_ed, run + 1)
                link(dve.tensor_scalar(mx[0][:, 0:jg], ed[:, 0, 0:jg], 2.0, 2.0, ALU.mult, ALU.add))
                link(dve.reciprocal(mx[1][:, 0:jg], mx[0][:, 0:jg]))
                link(dve.tensor_scalar(wts[:, 0, js], mx[1][:, 0:jg], 1.0 / WS, None, ALU.mult))
                dve.tensor_tensor(wts[:, 1, js], wts[:, 0, js], ed[:, 0, 0:jg], ALU.mult)

            def weights():
                dve.wait_ge(s_small, 16 * 3)
                dve.wait_ge(s_wexp, 1)
                dve.tensor_scalar(omix[:], vecs[:, 0:3], -1.0, 1.0, ALU.mult, ALU.add)
                link(dve.tensor_scalar(wdec[:, 0:1], wdec[:, 0:1], -1.0, None, ALU.mult))
                dve.tensor_tensor(wdec[:, 1:2], wdec[:, 0:1], vecs[:, 4:5], ALU.add)
                dve.tensor_scalar(wfull[:], wfull[:], wdec[:, 0:1], None, ALU.add)
                for i in range(3):
                    dve.tensor_scalar(qkv_f[:, i, :], att_raw[:, i, :], vecs[:, i:i + 1], None, ALU.mult)
                    ins = dve.tensor_scalar(qkv_f[:, 3 + i, :], att_raw[:, i, :], omix[:, i:i + 1], None, ALU.mult)
                ins.then_inc(s_qf, 1)
                with dve.Fori(0, E // WRING) as i:
                    for k in range(WRING):
                        e = i * WRING + k
                        dve.wait_ge(s_uphi, e + 1)
                        dve.scalar_tensor_tensor(
                            up_w[:, bass.ds(e, 1), 1::2, :].rearrange("p e a f -> p (e a) f"), stage_w[:, :, k, :], WS,
                            up_w[:, bass.ds(e, 1), 0::2, :].rearrange("p e a f -> p (e a) f"),
                            ALU.mult, ALU.subtract).then_inc(s_uplo, 1)
                dve.wait_ge(s_qf, 1)
                dve.wait_ge(s_qhi, 1)
                dve.scalar_tensor_tensor(qkv_w[:, :, 1, :], qkv_f[:], WS, qkv_w[:, :, 0, :],
                                         ALU.mult, ALU.subtract).then_inc(s_qlo, 1)

            def half(n, k):
                dve.wait_ge(s_sil, n + 1)
                wait(dve, s_y, n - RING + 1)
                dve.tensor_tensor(h[:, k, :, :].rearrange("p c t -> p (c t)"), sil[:, k % 2, :], pb[k % 2][:],
                                  ALU.mult).then_inc(s_h, 1)

            def combine(run, b):
                g, (u, js) = run % GROUPS, units(run, b)
                runs = [p[2] for p in PLAN if p[1] == "gather" and p[3] == b]
                dve.wait_ge(s_gat[b], 16 * TOPK * JU * (runs.index(run) + 1))
                for c in range(TOPK):
                    for j in range(JU):
                        xj = xres[:, js, :][:, j, :]
                        ins = dve.scalar_tensor_tensor(xj, yg[:, b, c, j, :], wts[:, c, u * JU + j:u * JU + j + 1],
                                                       xj, ALU.mult, ALU.add)
                    if c == 0:
                        link(ins)
                ins.then_inc(s_comb, 1)
                dve.wait_ge(s_comb, count(("combine",), ("combine", run, b)))

            def step(name, run, b):
                u, _ = units(run, b)
                k, v, r = kk[:, u % 2, :], vv[:, u % 2, :], tr[:, u % 2, :]
                if name == "combine":
                    combine(run, b)
                if name in ("stats", "mstats"):
                    if name == "stats" and run < GROUPS:
                        dve.wait_ge(s_x[run], 16 * (UNITS[0] if run == 0 else 1))
                    statistics(run, b)
                if name in ("rsqrt", "mrsqrt"):
                    rsqrt(slice(u, u + 1) if name == "mrsqrt" or run else slice(0, UNITS[0]))
                if name in NORMS:
                    normalise(name, run, b)
                if name in ("lo", "lo_m"):
                    parts_lo(name, run, b)
                if name == "pick":
                    pick_expert(run, 0)
                if name == "pick2":
                    pick_expert(run, 1)
                if name == "place":
                    place(run)
                if name == "place2":
                    place2(run)
                if name == "tiles":
                    tiles(run)
                if name == "weights":
                    expert_weights(run)
                if name == "peak":
                    dve.wait_ge(s_bread, count(B_STEPS, ("pk", run, b)))
                    link(dve.tensor_tensor_scan(pp[:, 1:], wfull[:], k, NEG, ALU.add, ALU.max))
                    link(dve.scalar_tensor_tensor(dd[:], pp[:, 0:S], vecs[:, 4:5], k, ALU.subtract, ALU.subtract))
                if name == "gaps":
                    wait(dve, s_exp, count(("exps2",), ("exps2", run, b)) - 1)
                    dve.tensor_scalar(mn[:, 0, :], dd[:], 0.0, None, ALU.min)
                    dve.tensor_scalar(mxx[:, 0, :], dd[:], 0.0, None, ALU.max)
                    dve.tensor_scalar(mn[:, 1, :], dd[:], wdec[:, 1:2], 0.0, ALU.add, ALU.min)
                    dve.tensor_scalar(mxx[:, 1, :], dd[:], wdec[:, 1:2], 0.0, ALU.add, ALU.max).then_inc(s_min, 1)
                if name == "sum_a":
                    dve.wait_ge(s_exp, count(("exps2",), ("exps2", run, b)))
                    dve.wait_ge(s_aread, count(A_STEPS, ("pv", run, b)))
                    link(dve.tensor_tensor(kv[:], e2[:, 1, :], v, ALU.mult))
                    link(dve.tensor_tensor_scan(aa[:, 1:], e1[:, 1, :], kv[:], 0.0, ALU.mult, ALU.add))
                if name == "sum_b":
                    link(dve.tensor_tensor_scan(bb[:, 1:], e1[:, 1, :], e2[:, 1, :], 0.0, ALU.mult, ALU.add))
                    dve.tensor_tensor(num[:], e1[:, 0, :], aa[:, 0:S], ALU.mult)
                if name == "weigh":
                    dve.tensor_tensor(tm[:], e2[:, 0, :], v, ALU.mult)
                    link(dve.tensor_tensor(den[:], e1[:, 0, :], bb[:, 0:S], ALU.mult))
                if name == "total":
                    dve.tensor_tensor(num[:], num[:], tm[:], ALU.add)
                    dve.tensor_tensor(den[:], den[:], e2[:, 0, :], ALU.add).then_inc(s_sums, 1)
                    dve.wait_ge(s_sums, count(("total",), ("total", run, b)))
                if name == "divide":
                    dve.wait_ge(s_bread, count(B_STEPS, ("pr", run, b)))
                    dve.scalar_tensor_tensor(num[:], r, 1.0, num[:], ALU.add, ALU.mult)
                    link(dve.reciprocal(tm[:, 0:S // 4], den[:, 0:S // 4]))
                if name == "divide2":
                    link(dve.reciprocal(tm[:, S // 4:3 * S // 4], den[:, S // 4:3 * S // 4]))
                if name == "att":
                    link(dve.reciprocal(tm[:, 3 * S // 4:], den[:, 3 * S // 4:]))
                    dve.tensor_tensor(att[:], num[:], tm[:], ALU.mult).then_inc(s_att, 1)
                if name == "add":
                    u, js = units(run, b)
                    at = count(A_STEPS, ("out", run, b))
                    dve.wait_ge(s_afull, at)
                    dve.tensor_tensor(xres[:, js, :], xres[:, js, :], bkA[:].rearrange("p (j d) -> p j d", d=D),
                                      ALU.add).then_inc(s_aread, 1)
                    dve.wait_ge(s_aread, at)

            in_order(dve, half, step, before_halves=weights, halves=HALVES)
            last_steps(step)

        @block.tensor
        def _(pe):
            pe.wait_ge(s_const, 7)
            up_bytes = up_w[:].rearrange("p e a f -> p (e a f)").bitcast(U8)
            down_bytes = down_w[:].rearrange("p e c d -> p (e c d)").bitcast(U8)

            def turn_tile(t, slot):
                loads = t // SLOTS + 1 if isinstance(t, int) else (t - slot) // SLOTS + 1
                pe.wait_ge(s_rin[slot], 16 * loads)
                wait(pe, s_rT, t)
                for part in range(2):
                    for hh in range(TH):
                        mm = pe.transpose(pT[:, part, hh * P:(hh + 1) * P],
                                          rin[:, slot, hh, part * D:(part + 1) * D], ident16[:])
                mm.then_inc(s_turn, 1)

            def up_chunk(k, c, e):
                for bank, w in ((pa[k % 2], 0), (pb[k % 2], 2)):
                    for i, (wp, xp) in enumerate(((0, 0), (0, 1), (1, 0))):
                        at = 2 * ((w + wp) * F + (k % 2 * (FC // 2) + c) * P)
                        mm = pe.matmul(bank[:, c * T:(c + 1) * T],
                                       up_bytes[:, bass.ds(e * (2 * 4 * F) + at, 2 * P)].bitcast(F16),
                                       rT[:, k // 2, xp, :], start=(i == 0), stop=(i == 2))
                return mm

            def down(n, k, e):
                pe.wait_ge(s_h, n + 1)
                if k % 2 == 0:
                    wait(pe, s_yrow, tile_of(n, k)[0])
                for c in range(FC // 2):
                    at = 4 * (k % 2 * (FC // 2) + c) * D
                    w = down_bytes[:, bass.ds(e * (4 * FC * D) + at, 4 * D)].bitcast(F32)
                    for hh in range(TH):
                        mm = pe.matmul(py[:, hh, :], h[:, k, c, hh * P:(hh + 1) * P], w,
                                       start=(k % 2 == 0 and c == 0 and hh == 0),
                                       stop=(k % 2 == 1 and c == FC // 2 - 1), skip_group_check=True)
                mm.then_inc(s_y, 1)

            experts = [None] * SLOTS

            def load_expert(t, slot):
                both = pe.value_load(eid[0:1, bass.ds(t, 1)], min_val=0, max_val=E * E - 1)
                experts[slot] = pe.snap(both % E, min_val=0, max_val=E - 1)
                return both

            def half(n, k):
                t, slot = tile_of(n, k)
                looped = not isinstance(n, int)
                if not looped and k % 2 == 0 and t in START:
                    pe.wait_ge(s_eid, START.index(t) + 1)
                if k % 2 == 0 and not (looped and k == 2):
                    both = load_expert(t, slot)
                    if looped or n == HALVES - RING:
                        experts[-1] = pe.snap(both // E, min_val=0, max_val=E - 1)
                if k % 2 == 0:
                    pe.wait_ge(s_rT, t + 1)
                wait(pe, s_h, n - 1)
                up_chunk(k, 0, experts[slot])
                if k % 2 == 0 and not (isinstance(n, int) and n == HALVES - 2):
                    turn_tile(t + 1, (slot + 1) % SLOTS)
                up_chunk(k, 1, experts[slot]).then_inc(s_up, 1)
                if looped and k == 1:
                    nxt = pe.value_load(eid[0:1, bass.ds(t + 1, 1)], min_val=0, max_val=E * E - 1)
                if not (isinstance(n, int) and n < 2):
                    down(n - 2, (k - 2) % RING, experts[slot - 1])
                if looped and k == 1:
                    experts[1] = pe.snap(nxt % E, min_val=0, max_val=E - 1)

            def bank_free(s_read, uses):
                wait(pe, s_read, uses - 1)

            def project(u, i, bank):
                n = 0
                for f, start in ((i, 2), (3 + i, 1)):
                    for wp, xp in ((0, 0), (0, 1), (1, 0)):
                        mm = pe.matmul(bank[:], qkv_w[:, f, wp, :], xT[:, u % 2, xp, start:start + S],
                                       start=(n == 0), stop=(n == 5))
                        n += 1
                return mm

            def step(name, run, b):
                u, js = units(run, b)
                me = (name, run, b)
                if name in A_STEPS:
                    bank_free(s_aread, count(A_STEPS, me))
                if name in B_STEPS:
                    bank_free(s_bread, count(B_STEPS, me))
                if name == "turn":
                    pe.wait_ge(s_xn, count(NORMS, ("norm", run, b)))
                    for j in range(JU):
                        mm = pe.transpose(bkA[:, j * P:(j + 1) * P], xn[:, xn_slot("norm", run, b), j, :], ident[:])
                    mm.then_inc(s_afull, 1)
                if name == "logits":
                    pe.wait_ge(s_small, 16 * 3)
                    pe.wait_ge(s_aread, count(A_STEPS, ("turn", run, b)))
                    for j in range(JU):
                        mm = pe.matmul(bkB[:, j * E:(j + 1) * E], xnT[:, j * P:(j + 1) * P], gate_w[:],
                                       start=True, stop=True)
                    mm.then_inc(s_bfull, 1)
                if name == "count":
                    pe.wait_ge(s_chosen, run + 1)
                    cols = UNITS[run % GROUPS] * JU * E
                    cv = chosen[:].rearrange("p j e -> p (j e)")[:, 0:cols]
                    pe.matmul(bkB[:, 0:cols], ones16[:], cv, start=True, stop=True).then_inc(s_bfull, 1)
                    pe.matmul(bkA[:, 0:cols], upper[:], cv, start=True, stop=True).then_inc(s_afull, 1)
                if name == "turn_m":
                    pe.wait_ge(s_lo, count(("lo", "lo_m"), ("lo_m", run, b)))
                    a16 = bkA[:].bitcast(F16)
                    for part in range(2):
                        for j in range(JU):
                            mm = pe.transpose(a16[:, part * S + j * P:part * S + (j + 1) * P],
                                              parts[:, u * JU + j, part * D:(part + 1) * D], ident16[:])
                    mm.then_inc(s_afull, 1)
                if name == "pk":
                    pe.wait_ge(s_qlo, 1)
                    pe.wait_ge(s_aread, count(A_STEPS, ("turn_m", run, b)))
                    project(u, 0, bkB).then_inc(s_bfull, 1)
                if name == "pv":
                    project(u, 1, bkA).then_inc(s_afull, 1)
                if name == "pr":
                    project(u, 2, bkB).then_inc(s_bfull, 1)
                if name == "out":
                    pe.wait_ge(s_att, count(("att",), ("att", run, b)))
                    for j in range(JU):
                        mm = pe.matmul(bkA[:, j * P:(j + 1) * P], att[:, j * P:(j + 1) * P], att_raw[:, 3, :],
                                       start=True, stop=True)
                    mm.then_inc(s_afull, 1)

            def weights_in():
                turn_tile(0, 0)
                pe.wait_ge(s_uplo, E)
                pe.wait_ge(s_w2, 16)

            in_order(pe, half, step, before_halves=weights_in, halves=HALVES - RING)
            for n in range(HALVES - RING, HALVES):
                half(n, n % RING)
            for n in range(HALVES - 2, HALVES):
                down(n, n % RING, experts[(TILES - 1) % SLOTS])


def kernel(L0_attn_x, L0_attn_time_mix_k, L0_attn_time_mix_v, L0_attn_time_mix_r, L0_attn_time_decay,
           L0_attn_time_first, L0_attn_Wk, L0_attn_Wv, L0_attn_Wr, L0_attn_Wo, L0_ffn_gate_w, L0_ffn_w1,
           L0_ffn_w3, L0_ffn_w2):
    import numpy as np
    import concourse.bacc as bacc
    from concourse.bass_utils import run_bass_kernel_spmd

    vec = [L0_attn_time_mix_k, L0_attn_time_mix_v, L0_attn_time_mix_r, L0_attn_time_decay, L0_attn_time_first]
    arrays = {
        "x": np.ascontiguousarray(L0_attn_x),
        "channel_vecs": np.ascontiguousarray(np.stack([np.asarray(v).reshape(D) for v in vec], axis=1)),
        "att_w": np.ascontiguousarray(np.stack(
            [np.asarray(w).T for w in (L0_attn_Wk, L0_attn_Wv, L0_attn_Wr, L0_attn_Wo)], axis=1)),
        "gate": np.ascontiguousarray(L0_ffn_gate_w),
        "w1": np.ascontiguousarray(L0_ffn_w1),
        "w3": np.ascontiguousarray(L0_ffn_w3),
        "w2": np.ascontiguousarray(L0_ffn_w2),
    }
    nc = bacc.Bacc("TRN2", target_bir_lowering=False, num_devices=1)
    args = [nc.dram_tensor(f"in_{n}", a.shape, mybir.dt.from_np(a.dtype), kind="ExternalInput").ap()
            for n, a in arrays.items()]
    out = nc.dram_tensor("out_0", (B, S, D), F32, kind="ExternalOutput").ap()
    macaron_kernel(nc, *args, out)
    r = run_bass_kernel_spmd(nc, [{f"in_{n}": a for n, a in arrays.items()}], core_ids=[0])
    return r.results[0]["out_0"]
```
